# Optimizing a Trainium2 kernel written in Bass

```python
import numpy as np
import jax
import jax.numpy as jnp

def _softmax(x, axis=-1):
    return jax.nn.softmax(x, axis=axis)

def _gelu(x):
    return jax.nn.gelu(x, approximate=True)

def _silu(x):
    return jax.nn.silu(x)

def _sigmoid(x):
    return jax.nn.sigmoid(x)

def _layernorm(x, axis=-1, eps=1e-05):
    m = jnp.mean(x, axis=axis, keepdims=True)
    v = jnp.var(x, axis=axis, keepdims=True)
    return (x - m) / jnp.sqrt(v + eps)

def _scatter_add(tgt, idx, src, axis=0):
    return tgt.at[idx].add(src)

def _segment_sum(src, seg, n):
    return jax.ops.segment_sum(src, seg, n)
kernel_name = 'mk_macaron_d2_jaxref_r4_6ea76e'

def setup_inputs(seed: int=0):
    np.random.seed(seed)
    _w = jnp.asarray

    def _L0_attn_setup():
        import jax, jax.numpy as jnp
        import numpy as np
        D_MODEL = 256
        N_HEADS = 16
        key = jax.random.key(seed)
        k1, k2, k3, k4 = jax.random.split(key, 4)
        B, T, D = (4, 512, D_MODEL)
        x = jax.random.normal(k1, (B, T, D), dtype=jnp.float32)
        w_qkv = jax.random.normal(k2, (D, 3 * D), dtype=jnp.float32) / np.sqrt(D)
        w_out = jax.random.normal(k3, (D, D), dtype=jnp.float32) / np.sqrt(D)
        b_out = jax.random.normal(k4, (D,), dtype=jnp.float32) * 0.01
        return {'x': x, 'w_qkv': w_qkv, 'w_out': w_out, 'b_out': b_out}
    _L0_attn_in = _L0_attn_setup()

    def _L0_ffn_setup():
        import jax, jax.numpy as jnp
        import numpy as np
        B, S, H = (4, 512, 256)
        E = 8
        GS = 2
        NG = E // GS
        F = int(H * 4 * (2.0 / 3.0))
        key = jax.random.key(seed)
        ks = jax.random.split(key, 7)
        sc_h = 1.0 / np.sqrt(H)
        sc_f = 1.0 / np.sqrt(F)
        return {'x': jax.random.normal(ks[0], (B, S, H), dtype=jnp.float32), 'Wr': jax.random.normal(ks[1], (H, E), dtype=jnp.float32) * sc_h, 'br': jnp.zeros((E,), dtype=jnp.float32), 'W_up': jax.random.normal(ks[2], (NG, H, F), dtype=jnp.float32) * sc_h, 'b_up': jax.random.normal(ks[3], (NG, F), dtype=jnp.float32) * 0.01, 'W_down': jax.random.normal(ks[4], (E, F, H), dtype=jnp.float32) * sc_f, 'b_down': jax.random.normal(ks[5], (E, H), dtype=jnp.float32) * 0.01}
    _L0_ffn_in = _L0_ffn_setup()

    def _L1_attn_setup():
        import jax, jax.numpy as jnp
        import numpy as np
        D_MODEL = 256
        D_INNER = 512
        D_STATE = 16
        D_CONV = 4
        DT_RANK = 64
        B_SZ = 2
        L_SEQ = 512
        EPS = 1e-06

        def _silu(v):
            return v * jax.nn.sigmoid(v)
        key = jax.random.key(seed)
        ks = jax.random.split(key, 9)

        def g(k, shape, scale=0.02):
            return jax.random.normal(k, shape, jnp.float32) * scale
        return {'x': jax.random.normal(ks[0], (B_SZ, L_SEQ, D_MODEL), jnp.float32), 'ln_gamma': jnp.ones((D_MODEL,), jnp.float32), 'ln_beta': jnp.zeros((D_MODEL,), jnp.float32), 'in_proj_w': g(ks[1], (2 * D_INNER, D_MODEL)), 'conv_w': g(ks[2], (D_INNER, 1, D_CONV), 0.1), 'conv_b': g(ks[3], (D_INNER,), 0.1), 'x_proj_w': g(ks[4], (DT_RANK + 2 * D_STATE, D_INNER)), 'dt_proj_w': g(ks[5], (D_INNER, DT_RANK), 0.1), 'dt_proj_b': g(ks[6], (D_INNER,), 0.1), 'A_log': jnp.log(jnp.broadcast_to(jnp.arange(1, D_STATE + 1, dtype=jnp.float32), (D_INNER, D_STATE))), 'D': jnp.ones((D_INNER,), jnp.float32), 'out_proj_w': g(ks[7], (D_MODEL, D_INNER))}
    _L1_attn_in = _L1_attn_setup()

    def _L1_ffn_setup():
        import jax, jax.numpy as jnp
        import numpy as np
        DIM = 256

        def _reference_tuple_inner(x, W_r, W_k, W_v, mu_r, mu_k):
            B, T, C = x.shape
            x_prev = jnp.concatenate([jnp.zeros((B, 1, C), x.dtype), x[:, :-1, :]], axis=1)
            xr = mu_r * x + (1.0 - mu_r) * x_prev
            xk = mu_k * x + (1.0 - mu_k) * x_prev
            r = jax.nn.sigmoid(jnp.einsum('btc,dc->btd', xr, W_r))
            k = jnp.einsum('btc,dc->btd', xk, W_k)
            k_act = jnp.square(jax.nn.relu(k))
            out = r * jnp.einsum('btc,dc->btd', k_act, W_v)
            new_state = x[:, -1, :]
            return (out, new_state)
        key = jax.random.key(seed)
        ks = jax.random.split(key, 6)
        B, T, C = (8, 512, DIM)
        x = jax.random.normal(ks[0], (B, T, C), dtype=jnp.float32)
        s = 1.0 / np.sqrt(C)
        W_r = jax.random.uniform(ks[1], (C, C), jnp.float32, -s, s)
        W_k = jax.random.uniform(ks[2], (C, C), jnp.float32, -s, s)
        W_v = jax.random.uniform(ks[3], (C, C), jnp.float32, -s, s)
        mu_r = jax.random.uniform(ks[4], (C,), jnp.float32)
        mu_k = jax.random.uniform(ks[5], (C,), jnp.float32)
        return {'x': x, 'W_r': W_r, 'W_k': W_k, 'W_v': W_v, 'mu_r': mu_r, 'mu_k': mu_k}
    _L1_ffn_in = _L1_ffn_setup()
    _d = {'L0_attn_x': _L0_attn_in['x'], 'L0_attn_w_qkv': _L0_attn_in['w_qkv'], 'L0_attn_w_out': _L0_attn_in['w_out'], 'L0_attn_b_out': _L0_attn_in['b_out'], 'L0_ffn_Wr': _L0_ffn_in['Wr'], 'L0_ffn_br': _L0_ffn_in['br'], 'L0_ffn_W_up': _L0_ffn_in['W_up'], 'L0_ffn_b_up': _L0_ffn_in['b_up'], 'L0_ffn_W_down': _L0_ffn_in['W_down'], 'L0_ffn_b_down': _L0_ffn_in['b_down'], 'L1_attn_ln_gamma': _L1_attn_in['ln_gamma'], 'L1_attn_ln_beta': _L1_attn_in['ln_beta'], 'L1_attn_in_proj_w': _L1_attn_in['in_proj_w'], 'L1_attn_conv_w': _L1_attn_in['conv_w'], 'L1_attn_conv_b': _L1_attn_in['conv_b'], 'L1_attn_x_proj_w': _L1_attn_in['x_proj_w'], 'L1_attn_dt_proj_w': _L1_attn_in['dt_proj_w'], 'L1_attn_dt_proj_b': _L1_attn_in['dt_proj_b'], 'L1_attn_A_log': _L1_attn_in['A_log'], 'L1_attn_D': _L1_attn_in['D'], 'L1_attn_out_proj_w': _L1_attn_in['out_proj_w'], 'L1_ffn_W_r': _L1_ffn_in['W_r'], 'L1_ffn_W_k': _L1_ffn_in['W_k'], 'L1_ffn_W_v': _L1_ffn_in['W_v'], 'L1_ffn_mu_r': _L1_ffn_in['mu_r'], 'L1_ffn_mu_k': _L1_ffn_in['mu_k']}
    _x0 = _d['L0_attn_x']
    _d['L0_attn_x'] = jax.random.normal(jax.random.fold_in(jax.random.key(seed), 1), (8, 1024, 256), dtype=_x0.dtype)
    del _x0
    return _d

def reference(L0_attn_x, L0_attn_w_qkv, L0_attn_w_out, L0_attn_b_out, L0_ffn_Wr, L0_ffn_br, L0_ffn_W_up, L0_ffn_b_up, L0_ffn_W_down, L0_ffn_b_down, L1_attn_ln_gamma, L1_attn_ln_beta, L1_attn_in_proj_w, L1_attn_conv_w, L1_attn_conv_b, L1_attn_x_proj_w, L1_attn_dt_proj_w, L1_attn_dt_proj_b, L1_attn_A_log, L1_attn_D, L1_attn_out_proj_w, L1_ffn_W_r, L1_ffn_W_k, L1_ffn_W_v, L1_ffn_mu_r, L1_ffn_mu_k):

    def _L0_attn_ref(x, w_qkv, w_out, b_out):
        import jax, jax.numpy as jnp
        import numpy as np
        D_MODEL = 256
        N_HEADS = 16
        B, T, D = x.shape
        h = N_HEADS
        Hd = D // h
        qkv = jnp.einsum('btd,de->bte', x, w_qkv).reshape(B, T, 3, h, Hd)
        q = jnp.transpose(qkv[:, :, 0], (0, 2, 1, 3))
        k = jnp.transpose(qkv[:, :, 1], (0, 2, 1, 3))
        v = jnp.transpose(qkv[:, :, 2], (0, 2, 1, 3))
        scale = 1.0 / jnp.sqrt(jnp.array(Hd, dtype=x.dtype))
        logits = jnp.einsum('bhqd,bhkd->bhqk', q, k) * scale
        mask = jnp.tril(jnp.ones((T, T), dtype=x.dtype))
        big_neg = jnp.array(-10000000000.0, dtype=x.dtype)
        logits = logits + (1.0 - mask)[None, None, :, :] * big_neg
        attn = jax.nn.softmax(logits, axis=-1)
        out = jnp.einsum('bhqk,bhkd->bhqd', attn, v)
        out = jnp.transpose(out, (0, 2, 1, 3)).reshape(B, T, D)
        return jnp.einsum('btd,de->bte', out, w_out) + b_out

    def _L0_ffn_ref(x, Wr, br, W_up, b_up, W_down, b_down):
        import jax, jax.numpy as jnp
        import numpy as np
        B, S, H = (4, 512, 256)
        E = 8
        GS = 2
        NG = E // GS
        F = int(H * 4 * (2.0 / 3.0))
        b, s, h = x.shape
        n_tok = b * s
        k = n_tok // E
        xf = x.reshape(n_tok, h)
        logits = xf @ Wr + br
        Sm = jax.nn.softmax(logits, axis=-1)
        G_t, idx_t = jax.lax.top_k(Sm.T, k)
        G = G_t.T
        idx = idx_t.T
        tokens = xf[idx]
        group = jnp.arange(E) // GS
        Wu = W_up[group]
        bu = b_up[group]
        mid = jax.nn.silu(jnp.einsum('keh,ehf->kef', tokens, Wu) + bu)
        out = jnp.einsum('kef,efh->keh', mid, W_down) + b_down
        y = jnp.zeros_like(xf).at[idx].add(G[..., None] * out)
        return y.reshape(b, s, h)

    def _L1_attn_ref(x, ln_gamma, ln_beta, in_proj_w, conv_w, conv_b, x_proj_w, dt_proj_w, dt_proj_b, A_log, D, out_proj_w):
        import jax, jax.numpy as jnp
        import numpy as np
        D_MODEL = 256
        D_INNER = 512
        D_STATE = 16
        D_CONV = 4
        DT_RANK = 64
        B_SZ = 2
        L_SEQ = 512
        EPS = 1e-06

        def _silu(v):
            return v * jax.nn.sigmoid(v)
        B, L, _ = x.shape
        mu = x.mean(-1, keepdims=True)
        var = x.var(-1, keepdims=True)
        h = (x - mu) / jnp.sqrt(var + EPS) * ln_gamma + ln_beta
        xz = jnp.einsum('bld,ed->bel', h, in_proj_w)
        u, z = jnp.split(xz, 2, axis=1)
        up = jnp.pad(u, ((0, 0), (0, 0), (D_CONV - 1, 0)))
        uc = jax.lax.conv_general_dilated(up, conv_w, (1,), 'VALID', dimension_numbers=('NCH', 'OIH', 'NCH'), feature_group_count=D_INNER)
        uc = _silu(uc + conv_b[None, :, None])
        x_dbl = jnp.einsum('bdl,ed->ble', uc, x_proj_w)
        dt, Bm, Cm = jnp.split(x_dbl, [DT_RANK, DT_RANK + D_STATE], axis=-1)
        delta = jnp.einsum('blr,dr->bdl', dt, dt_proj_w) + dt_proj_b[None, :, None]
        delta = jax.nn.softplus(delta)
        A = -jnp.exp(A_log)
        deltaA = jnp.exp(jnp.einsum('bdl,dn->bdln', delta, A))
        Bm = jnp.transpose(Bm, (0, 2, 1))
        Cm = jnp.transpose(Cm, (0, 2, 1))
        deltaB_u = jnp.einsum('bdl,bnl,bdl->bdln', delta, Bm, uc)

        def step(state, inp):
            dA, dBu, Ct = inp
            state = dA * state + dBu
            y = jnp.einsum('bdn,bn->bd', state, Ct)
            return (state, y)
        init = jnp.zeros((B, D_INNER, D_STATE), jnp.float32)
        _, ys = jax.lax.scan(step, init, (jnp.moveaxis(deltaA, 2, 0), jnp.moveaxis(deltaB_u, 2, 0), jnp.moveaxis(Cm, 2, 0)))
        y = jnp.moveaxis(ys, 0, 2)
        y = y + uc * D[None, :, None]
        y = y * _silu(z)
        out = jnp.einsum('bdl,ed->ble', y, out_proj_w)
        return out + x

    def _L1_ffn_ref(x, W_r, W_k, W_v, mu_r, mu_k):
        import jax, jax.numpy as jnp
        import numpy as np
        DIM = 256

        def _reference_tuple_inner(x, W_r, W_k, W_v, mu_r, mu_k):
            B, T, C = x.shape
            x_prev = jnp.concatenate([jnp.zeros((B, 1, C), x.dtype), x[:, :-1, :]], axis=1)
            xr = mu_r * x + (1.0 - mu_r) * x_prev
            xk = mu_k * x + (1.0 - mu_k) * x_prev
            r = jax.nn.sigmoid(jnp.einsum('btc,dc->btd', xr, W_r))
            k = jnp.einsum('btc,dc->btd', xk, W_k)
            k_act = jnp.square(jax.nn.relu(k))
            out = r * jnp.einsum('btc,dc->btd', k_act, W_v)
            new_state = x[:, -1, :]
            return (out, new_state)
        return _reference_tuple_inner(x, W_r, W_k, W_v, mu_r, mu_k)[0]
    x = L0_attn_x
    x = x + 0.5 * _L0_ffn_ref(_layernorm(x, axis=-1), L0_ffn_Wr, L0_ffn_br, L0_ffn_W_up, L0_ffn_b_up, L0_ffn_W_down, L0_ffn_b_down)
    x = x + _L0_attn_ref(_layernorm(x, axis=-1), L0_attn_w_qkv, L0_attn_w_out, L0_attn_b_out)
    x = x + 0.5 * _L0_ffn_ref(_layernorm(x, axis=-1), L0_ffn_Wr, L0_ffn_br, L0_ffn_W_up, L0_ffn_b_up, L0_ffn_W_down, L0_ffn_b_down)
    x = x + 0.5 * _L1_ffn_ref(_layernorm(x, axis=-1), L1_ffn_W_r, L1_ffn_W_k, L1_ffn_W_v, L1_ffn_mu_r, L1_ffn_mu_k)
    x = x + _L1_attn_ref(_layernorm(x, axis=-1), L1_attn_ln_gamma, L1_attn_ln_beta, L1_attn_in_proj_w, L1_attn_conv_w, L1_attn_conv_b, L1_attn_x_proj_w, L1_attn_dt_proj_w, L1_attn_dt_proj_b, L1_attn_A_log, L1_attn_D, L1_attn_out_proj_w)
    x = x + 0.5 * _L1_ffn_ref(_layernorm(x, axis=-1), L1_ffn_W_r, L1_ffn_W_k, L1_ffn_W_v, L1_ffn_mu_r, L1_ffn_mu_k)
    return x

_drawn_inputs = setup_inputs


def setup_inputs(seed=0):
    import zlib

    import numpy as np

    out = dict(_drawn_inputs(seed))
    spreads = {'L0_ffn_br': (0.0, 0.1),
     'L1_attn_ln_gamma': (1.0, 0.2),
     'L1_attn_ln_beta': (0.0, 0.1),
     'L1_attn_D': (1.0, 0.2)}
    factors = {}
    for name, (base, spread) in spreads.items():
        noise = np.random.default_rng([zlib.crc32(name.encode()), seed]).standard_normal(out[name].shape)
        drawn = base * np.exp(spread * noise) if base else spread * noise
        out[name] = jnp.asarray(drawn.astype(out[name].dtype))
    for name, factor in factors.items():
        out[name] = (out[name] * factor).astype(out[name].dtype)
    return out
```

```python
import concourse.bass as bass
from concourse import mybir
from contextlib import ExitStack

fp32 = mybir.dt.float32
bf16 = mybir.dt.bfloat16
i32 = mybir.dt.int32
ACT = mybir.ActivationFunctionType
ALU = mybir.AluOpType
AX = mybir.AxisListType

P = 128
B, L, D = 8, 1024, 256
N_TOK = B * L
LT = L // P
DH = D // P
TILES = N_TOK // P
BANK = 512
EPS = 1e-5
E, GS, F = 8, 2, 682
CAP = N_TOK // E
NG = E // GS
FT = 6
FR = F - (FT - 1) * P
ROW = D + E


def hold(eng, sem, value, passed):
    eng.wait_ge(sem, value)
    eng.sem_inc(passed, 1)


class Link:

    def __init__(self, eng, sem):
        self.eng, self.sem, self.base, self.n = eng, sem, 0, 0

    def at(self, base):
        self.base, self.n = base, 0

    def inc(self, ins):
        ins.then_inc(self.sem, 1)
        self.n += 1
        return self.base + self.n

    def wait(self):
        self.eng.wait_ge(self.sem, self.base + self.n)

    def step(self, ins):
        self.inc(ins)
        self.wait()


class Pool_:

    def __init__(self, nc, ctx, stage):
        self.nc, self.ctx, self.stage, self.all_sems = nc, ctx, stage, []
        ctx.callback(self.clear)

    def clear(self):
        if self.all_sems:
            self.nc.clear_and_free_semaphores(self.all_sems)
            self.nc.all_engine_barrier()

    def sb(self, name, shape, dt=fp32):
        return self.ctx.enter_context(self.nc.sbuf_tensor(f"{self.stage}_{name}", shape, dt))

    def ps(self, name, shape, dt=fp32):
        return self.ctx.enter_context(self.nc.psum_tensor(f"{self.stage}_{name}", shape, dt))

    def sem(self, name):
        self.all_sems.append(self.nc.alloc_semaphore(f"{self.stage}_{name}"))
        return self.all_sems[-1]

    def sems(self, name, n=2):
        return [self.sem(f"{name}{u}") for u in range(n)]


def rows(x, i):
    return x.rearrange("(b t p) d -> b p t d", t=LT, p=P)[i]


def norm_stats(dve, link, x, stats, mv, stats_ready, passed):
    for t in range(LT):
        link.inc(dve.bn_stats(stats[:, t, :], x[:, t, :]))
    hold(dve, link.sem, link.base + link.n, passed)
    for t in range(LT):
        ins = dve.bn_aggr(mv[:, t, :], stats[:, t, :])
    ins.then_inc(stats_ready, 1)


def norm_rstd(pool, link, mv, veps, rstd, neg_half, eps, rstd_ready):
    link.step(pool.tensor_scalar(veps[:, :], mv[:, :, 1], eps, None, ALU.add))
    pool.tensor_tensor(rstd[:, :], veps[:, :], neg_half[:, 0:LT], ALU.pow).then_inc(rstd_ready, 1)


def norm_apply(dve, x, mv, rstd, xn, xn_ready):
    for t in range(LT):
        ins = dve.tensor_scalar(xn[:, t, :], x[:, t, :], mv[:, t, 0:1], rstd[:, t:t + 1],
                                ALU.subtract, ALU.mult)
    ins.then_inc(xn_ready, 1)


def transposes(pe, x, psT, ident, psT_used, psT_ready, count):
    for k in range(2 * DH):
        h, q = k // 2, k % 2
        pe.wait_ge(psT_used[k % 2], count + k // 2)
        for j in range(4):
            ins = pe.transpose(psT[k % 2][:, j * P:(j + 1) * P],
                               x[:, 4 * q + j, h * P:(h + 1) * P], ident[:, :])
        ins.then_inc(psT_ready[k % 2], 1)



def moe(nc, tag, x_in, x_out, xn_dram, st_dram, Wr, br, Wup, bup, Wdown, bdown, consts):
    with ExitStack() as ctx:
        a = Pool_(nc, ctx, tag)
        logit = a.sb("logit", [P, TILES, E])
        slots = a.sb("slots", [P, E, 8], i32)
        moe_router(nc, tag + "r", x_in, x_out, xn_dram, Wr, br, consts, logit)
        moe_choose(nc, tag + "c", xn_dram, st_dram, consts, logit, slots)
        moe_ffn(nc, tag + "f", x_out, xn_dram, Wup, bup, Wdown, bdown, consts, slots)


def moe_router(nc, tag, x_in, x_out, xn_dram, Wr, br, consts, logit):
    with ExitStack() as ctx:
        a = Pool_(nc, ctx, tag)
        ident = a.sb("ident", [P, P])
        wr = a.sb("wr", [P, DH, E])
        brb = a.sb("brb", [P, E])
        neg_half = a.sb("neg_half", [P, LT])
        xt = [a.sb(f"xt{u}", [P, LT, D]) for u in range(2)]
        xn = [a.sb(f"xn{u}", [P, LT, D]) for u in range(2)]
        xT = [a.sb(f"xT{u}", [P, DH, L]) for u in range(2)]
        stats = [a.sb(f"stats{u}", [P, LT, 6]) for u in range(2)]
        mv = [a.sb(f"mv{u}", [P, LT, 2]) for u in range(2)]
        veps = [a.sb(f"veps{u}", [P, LT]) for u in range(2)]
        rstd = [a.sb(f"rstd{u}", [P, LT]) for u in range(2)]
        psT = [a.ps(f"psT{k}", [P, BANK]) for k in range(2)]
        psL = [a.ps(f"psL{u}", [P, LT, E]) for u in range(2)]

        consts_loaded = a.sem("consts_loaded")
        x_loaded = a.sems("x_loaded")
        xn_stored, x_stored = a.sems("xn_stored"), a.sems("x_stored")
        stats_ready, rstd_ready = a.sem("stats_ready"), a.sem("rstd_ready")
        xn_ready, psT_ready, psT_used = a.sem("xn_ready"), a.sems("psT_ready"), a.sems("psT_used")
        logit_ps, logit_ready = a.sem("logit_ps"), a.sem("logit_ready")
        d_step, g_step, passed = a.sem("d_step"), a.sem("g_step"), a.sem("passed")

        with nc.Block() as block:
            @block.sync
            def _(sp):
                for dst, src in ((ident[:, :], consts["ident"]),
                                 (wr[:, :, :], Wr.rearrange("(h p) e -> p h e", p=P)),
                                 (brb[:, :], br.rearrange("(o e) -> o e", o=1).to_broadcast([P, E]))):
                    sp.dma_start(dst, src).then_inc(consts_loaded, 16)
                with sp.Fori(0, B // 2) as i:
                    for u in range(2):
                        sp.wait_ge(xn_stored[u], 16 * i)
                        sp.wait_ge(x_stored[u], 16 * i)
                        sp.dma_start(xt[u][:, :, :], rows(x_in, 2 * i + u)).then_inc(x_loaded[u], 16)

            @block.scalar
            def _(act):
                with act.Fori(0, B // 2) as i:
                    for u in range(2):
                        act.wait_ge(x_loaded[u], 16 * i + 16)
                        act.dma_start(rows(x_out, 2 * i + u), xt[u][:, :, :]).then_inc(x_stored[u], 16)
                        act.wait_ge(xn_ready, 2 * i + u + 1)
                        act.dma_start(rows(xn_dram, 2 * i + u)[:, :, 0:D], xn[u][:, :, :]).then_inc(xn_stored[u], 16)
                        act.wait_ge(logit_ps, 2 * i if u == 0 else 2 * i)
                        for k in range(2 * DH):
                            h, q = k // 2, k % 2
                            act.wait_ge(psT_ready[k % 2], 4 * i + 2 * u + k // 2 + 1)
                            act.copy(xT[u][:, h, q * BANK:(q + 1) * BANK], psT[k % 2][:, :]).then_inc(
                                psT_used[k % 2], 1)
                for u in range(2):
                    act.wait_ge(xn_stored[u], 16 * (B // 2))
                    act.wait_ge(x_stored[u], 16 * (B // 2))

            @block.gpsimd
            def _(pool):
                link = Link(pool, g_step)
                link.step(pool.memset(neg_half[:, :], -0.5))
                with pool.Fori(0, B // 2) as i:
                    for u in range(2):
                        link.at(2 * i + u + 1)
                        hold(pool, stats_ready, 2 * i + u + 1, passed)
                        norm_rstd(pool, link, mv[u], veps[u], rstd[u], neg_half, EPS, rstd_ready)

            @block.tensor
            def _(pe):
                pe.wait_ge(consts_loaded, 16 * 3)
                with pe.Fori(0, B // 2) as i:
                    for u in range(2):
                        pe.wait_ge(xn_ready, 2 * i + u + 1)
                        transposes(pe, xn[u], psT, ident, psT_used, psT_ready, 4 * i + 2 * u)
                        for k in range(2):
                            pe.wait_ge(psT_used[k], 4 * i + 2 * u + 2)
                        pe.wait_ge(logit_ready, 2 * i)
                        for t in range(LT):
                            for h in range(DH):
                                ins = pe.matmul(psL[u][:, t, :], xT[u][:, h, t * P:(t + 1) * P], wr[:, h, :],
                                                start=(h == 0), stop=(h == DH - 1))
                        ins.then_inc(logit_ps, 1)

            @block.vector
            def _(dve):
                link = Link(dve, d_step)
                dve.wait_ge(consts_loaded, 16 * 3)
                with dve.Fori(0, B // 2) as i:
                    for u in range(2):
                        n = 2 * i + u
                        link.at(n * LT)
                        dve.wait_ge(x_loaded[u], 16 * i + 16)
                        norm_stats(dve, link, xt[u], stats[u], mv[u], stats_ready, passed)
                        dve.wait_ge(rstd_ready, n + 1)
                        dve.wait_ge(stats_ready, n + 1)
                        dve.wait_ge(xn_stored[u], 16 * i)
                        dve.wait_ge(psT_ready[1], 4 * i + 2 * u)
                        norm_apply(dve, xt[u], mv[u], rstd[u], xn[u], xn_ready)
                        dve.wait_ge(logit_ps, n + 1)
                        dve.tensor_tensor(logit[:, bass.ds(n * LT, LT), :], psL[u][:, :, :],
                                          brb[:, :].rearrange("p (o e) -> p o e", o=1).to_broadcast([P, LT, E]),
                                          ALU.add).then_inc(logit_ready, 1)


def moe_choose(nc, tag, xn_dram, st_dram, consts, logit, slots):
    with ExitStack() as ctx:
        a = Pool_(nc, ctx, tag)
        ident = a.sb("ident", [P, P])
        same16 = a.sb("same16", [P, P])
        below16 = a.sb("below16", [P, P])
        pcol = a.sb("pcol", [P, 1])
        trow = a.sb("trow", [P, 512], bf16)
        mx = a.sb("mx", [P, TILES])
        den = a.sb("den", [P, TILES])
        rden = a.sb("rden", [P, TILES])
        S = a.sb("S", [P, E, TILES])
        Srow = a.sb("Srow", [P, TILES, E])
        SvT = a.sb("SvT", [P, 4, P])
        V = a.sb("V", [P, 512])
        T = a.sb("T", [P, 1], i32)
        cand = a.sb("cand", [P, 1], i32)
        take = a.sb("take", [P, 1], i32)
        cnt = a.sb("cnt", [P, 1])
        junk = a.sb("junk", [P, 512])
        ones = a.sb("ones", [P, 512])
        gt = a.sb("gt", [P, 512])
        eq = a.sb("eq", [P, 512])
        sg = a.sb("sg", [P, 512])
        se = a.sb("se", [P, 512])
        tot = a.sb("tot", [P, 2])
        off = a.sb("off", [P, 4])
        posi = a.sb("posi", [P, 512], i32)
        hi_i = a.sb("hi_i", [P, 512], i32)
        lo_i = a.sb("lo_i", [P, 512], i32)
        hi = a.sb("hi", [P, 512], bf16)
        lo = a.sb("lo", [P, 512], bf16)
        H = a.sb("H", [P, P, 512], bf16)
        LW = a.sb("LW", [P, 16, 512], bf16)
        idf = a.sb("idf", [P, E, 8])
        psV = a.ps("psV", [P, 4, P])
        psC = a.ps("psC", [P, 8])
        psI = a.ps("psI", [P, E, 8, 2])
        consts_loaded = a.sem("consts_loaded")
        shifted, exped = a.sem("shifted"), a.sem("exped")
        s_ready, s_stored = a.sem("s_ready"), a.sem("s_stored")
        v_ps, v_copied, v_stored, v_loaded = (a.sem(n) for n in ("v_ps", "v_copied", "v_stored", "v_loaded"))
        cnt_ready, cnt_sum = a.sem("cnt_ready"), a.sem("cnt_sum")
        pos_ready, posT_ready = a.sem("pos_ready"), a.sem("posT_ready")
        hot_ready, idx_ps = a.sem("hot_ready"), a.sem("idx_ps")
        d_step = a.sem("d_step")
        STEPS = 30

        with nc.Block() as block:
            @block.sync
            def _(sp):
                for dst, src in ((ident[:, :], consts["ident"]), (same16[:, :], consts["same16"]),
                                 (below16[:, :], consts["below16"]), (pcol[:, :], consts["pcol"]),
                                 (trow[:, :], consts["trow"])):
                    sp.dma_start(dst, src).then_inc(consts_loaded, 16)
                sp.wait_ge(s_ready, 1)
                sp.dma_start(xn_dram.rearrange("(t p) r -> p t r", p=P)[:, :, D:ROW],
                             Srow[:, :, :]).then_inc(s_stored, 16)
                sp.wait_ge(v_copied, 1)
                sp.dma_start(st_dram.rearrange("(h q c) (s p) -> (q c s) h p", h=4, q=2, s=4),
                             SvT[:, :, :]).then_inc(v_stored, 16)
                sp.wait_ge(v_stored, 16)
                sp.dma_start(V[:, :], st_dram).then_inc(v_loaded, 16)
                sp.wait_ge(s_stored, 16)

            @block.scalar
            def _(act):
                act.wait_ge(shifted, 1)
                act.activation(logit[:, :, :], logit[:, :, :], ACT.Exp).then_inc(exped, 1)

            @block.tensor
            def _(pe):
                pe.wait_ge(consts_loaded, 16 * 5)
                pe.wait_ge(s_ready, 1)
                for h in range(4):
                    ins = pe.transpose(psV[:, h, :], S[:, 2 * h:2 * h + 2, :].rearrange("p e t -> p (e t)"),
                                       ident[:, :])
                ins.then_inc(v_ps, 1)
                for k in range(STEPS):
                    pe.wait_ge(cnt_ready, k + 1)
                    pe.matmul(psC[:, 0:1], same16[:, :], cnt[:, :], start=True, stop=True).then_inc(cnt_sum, 1)
                pe.wait_ge(cnt_ready, STEPS + 1)
                pe.matmul(psC[:, 2:4], below16[:, :], tot[:, :], start=True, stop=True)
                pe.matmul(psC[:, 4:6], same16[:, :], tot[:, :], start=True, stop=True).then_inc(cnt_sum, 1)
                pe.wait_ge(pos_ready, 1)
                for s in range(4):
                    ins = pe.transpose(psV[:, s, :], junk[:, s * P:(s + 1) * P], ident[:, :])
                ins.then_inc(posT_ready, 1)
                pe.wait_ge(hot_ready, 1)
                for e in range(E):
                    for k in range(TILES):
                        s, c = k % 4, k // 4
                        col = (s * E + e) * 16 + c
                        ins = pe.matmul(psI[:, e, :, :].rearrange("p v w -> p (v w)"), H[:, :, col], LW[:, :, col],
                                        start=(k == 0), stop=(k == TILES - 1))
                ins.then_inc(idx_ps, 1)

            @block.vector
            def _(dve):
                link = Link(dve, d_step)
                dve.wait_ge(consts_loaded, 16 * 5)
                bc = lambda v: v[:, :].rearrange("p (t o) -> p t o", o=1).to_broadcast([P, TILES, E])
                link.step(dve.tensor_reduce(mx[:, :], logit[:, :, :], AX.X, ALU.max))
                dve.tensor_tensor(logit[:, :, :], logit[:, :, :], bc(mx), ALU.subtract).then_inc(shifted, 1)
                dve.wait_ge(exped, 1)
                link.step(dve.tensor_reduce(den[:, :], logit[:, :, :], AX.X, ALU.add))
                link.step(dve.reciprocal(rden[:, :], den[:, :]))
                link.step(dve.tensor_tensor(Srow[:, :, :], logit[:, :, :], bc(rden), ALU.mult))
                dve.tensor_copy(S[:, :, :].rearrange("p e t -> p t e"), Srow[:, :, :]).then_inc(s_ready, 1)
                dve.wait_ge(v_ps, 1)
                dve.tensor_copy(SvT[:, :, :], psV[:, :, :]).then_inc(v_copied, 1)
                link.inc(dve.memset(ones[:, :], 1.0))
                link.inc(dve.memset(T[:, :], 0))
                link.step(dve.memset(cand[:, :], 1 << (STEPS - 1)))
                dve.wait_ge(v_loaded, 16)
                for k in range(STEPS):
                    bit = STEPS - 1 - k
                    dve.tensor_scalar(junk[:, :], V[:, :], cand[:, :].bitcast(fp32), 0.0, ALU.is_ge, ALU.add,
                                      accum_out=cnt[:, :]).then_inc(cnt_ready, 1)
                    dve.wait_ge(cnt_sum, k + 1)
                    link.step(dve.tensor_scalar(take[:, :], psC[:, 0:1], float(CAP), float(1 << bit),
                                                ALU.is_ge, ALU.mult))
                    if bit:
                        link.inc(dve.scalar_tensor_tensor(cand[:, :], T[:, :], 1 << (bit - 1), take[:, :],
                                                          ALU.bitwise_or, ALU.bitwise_or))
                    link.step(dve.tensor_tensor(T[:, :], T[:, :], take[:, :], ALU.bitwise_or))
                Tf = T[:, :].bitcast(fp32)
                link.inc(dve.tensor_scalar(gt[:, :], V[:, :], Tf, None, ALU.is_gt))
                dve.wait_ge(cnt_ready, STEPS)
                link.inc(dve.tensor_scalar(junk[:, :], V[:, :], Tf, 4096.0, ALU.is_lt, ALU.mult))
                link.step(dve.tensor_scalar(eq[:, :], V[:, :], Tf, None, ALU.is_equal))
                link.inc(dve.tensor_tensor_scan(sg[:, :], ones[:, :], gt[:, :], 0.0, ALU.mult, ALU.add))
                link.step(dve.tensor_tensor_scan(se[:, :], ones[:, :], eq[:, :], 0.0, ALU.mult, ALU.add))
                link.step(dve.tensor_copy(tot[:, 0:1], sg[:, 511:512]))
                dve.tensor_copy(tot[:, 1:2], se[:, 511:512]).then_inc(cnt_ready, 1)
                dve.wait_ge(cnt_sum, STEPS + 1)
                link.step(dve.tensor_copy(off[:, 0:4], psC[:, 2:6]))
                link.step(dve.tensor_tensor(off[:, 1:2], off[:, 1:2], off[:, 2:3], ALU.add))
                link.step(dve.tensor_scalar(off[:, 0:2], off[:, 0:2], -1.0, None, ALU.add))
                link.inc(dve.scalar_tensor_tensor(sg[:, :], sg[:, :], off[:, 0:1], gt[:, :], ALU.add, ALU.mult))
                link.step(dve.scalar_tensor_tensor(se[:, :], se[:, :], off[:, 1:2], eq[:, :], ALU.add, ALU.mult))
                link.step(dve.tensor_tensor(sg[:, :], sg[:, :], se[:, :], ALU.add))
                dve.tensor_tensor(junk[:, :], junk[:, :], sg[:, :], ALU.add).then_inc(pos_ready, 1)
                dve.wait_ge(posT_ready, 1)
                link.step(dve.tensor_copy(posi[:, :], psV[:, :, :].rearrange("p s q -> p (s q)")))
                link.inc(dve.tensor_scalar(hi_i[:, :], posi[:, :], 127, None, ALU.bitwise_and))
                link.step(dve.tensor_scalar(lo_i[:, :], posi[:, :], 7, None, ALU.logical_shift_right))
                link.inc(dve.tensor_copy(hi[:, :], hi_i[:, :]))
                link.step(dve.tensor_copy(lo[:, :], lo_i[:, :]))
                for v in range(8):
                    dve.tensor_scalar(LW[:, 2 * v, :], lo[:, :], float(v), pcol[:, :], ALU.is_equal, ALU.mult)
                    dve.scalar_tensor_tensor(LW[:, 2 * v + 1, :], lo[:, :], float(v),
                                             trow[:, :],
                                             ALU.is_equal, ALU.mult)
                for v in range(P):
                    ins = dve.tensor_scalar(H[:, v, :], hi[:, :], float(v), None, ALU.is_equal)
                ins.then_inc(hot_ready, 1)
                dve.wait_ge(idx_ps, 1)
                link.step(dve.tensor_copy(idf[:, :, :], psI[:, :, :, 0]))
                link.step(dve.scalar_tensor_tensor(slots[:, :, :], psI[:, :, :, 1], float(P), idf[:, :, :],
                                                   ALU.mult, ALU.add))


def moe_ffn(nc, tag, x_out, xn_dram, Wup, bup, Wdown, bdown, consts, slots):
    HALF, HT = 512, 4
    IT = 2 * GS
    with ExitStack() as ctx:
        a = Pool_(nc, ctx, tag)
        ident = a.sb("ident", [P, P])
        wup = a.sb("wup", [P, DH, F])
        bu_all = a.sb("bu_all", [P, NG, FT])
        bu = a.sb("bu", [P, FT])
        wdn = a.sb("wdn", [P, FT, D])
        idx = [a.sb(f"idx{x}", [P, 8], i32) for x in range(GS)]
        g = [a.sb(f"g{u}", [P, HT, ROW]) for u in range(2)]
        gT = [a.sb(f"gT{u}", [P, DH, HALF]) for u in range(2)]
        mid = [a.sb(f"mid{u}", [P, FT, HALF]) for u in range(2)]
        gate = [a.sb(f"gate{m}", [P, HT]) for m in range(IT)]
        y = [a.sb(f"y{u}", [P, HT, D]) for u in range(2)]
        psT = [a.ps(f"psT{k}", [P, BANK]) for k in range(2)]
        psU = [a.ps(f"psU{k}", [P, BANK]) for k in range(3)]
        psD = [a.ps(f"psD{k}", [P, BANK]) for k in range(2)]
        ident_loaded, bu_loaded, ones_ready = a.sem("ident_loaded"), a.sem("bu_loaded"), a.sem("ones_ready")
        wup_loaded, wdn_loaded = a.sem("wup_loaded"), a.sem("wdn_loaded")
        g_loaded = a.sems("g_loaded")
        idx_ready = a.sem("idx_ready")
        psT_ready, gT_ready = a.sem("psT_ready"), a.sem("gT_ready")
        up_ready, mid_ready = a.sem("up_ready"), a.sem("mid_ready")
        down_ready, y_ready, y_added = a.sem("down_ready"), a.sem("y_ready"), a.sem("y_added")
        gate_ready, bu_ready, passed = a.sem("gate_ready"), a.sem("bu_ready"), a.sem("passed")

        with nc.Block() as block:
            @block.sync
            def _(sp):
                sp.dma_start(ident[:, :], consts["ident"]).then_inc(ident_loaded, 16)
                sp.dma_start(bu_all[:, :, :].rearrange("p g f -> p (g f)"), bup).then_inc(bu_loaded, 16)
                with sp.Fori(0, NG) as i:
                    sp.wait_ge(up_ready, i * IT * FT)
                    sp.dma_start(wup[:, :, :], Wup.rearrange("g (h p) f -> g p h f", p=P)[i]).then_inc(wup_loaded, 16)
                    for x in range(GS):
                        sp.wait_ge(down_ready, (i * IT + 2 * x) * 2)
                        for dst, src in ((wdn[:, 0:FT - 1, :], Wdown[:, 0:(FT - 1) * P, :].rearrange("e (j p) d -> e p j d", p=P)),
                                         (wdn[0:FR, FT - 1, :], Wdown[:, (FT - 1) * P:F, :]),
                                         (wdn[FR:FR + 1, FT - 1, :], bdown.rearrange("e (o d) -> e o d", o=1))):
                            sp.dma_start(dst, src[GS * i + x]).then_inc(wdn_loaded, 16)

            @block.gpsimd
            def _(pool):
                pool.memset(mid[0][:, FT - 1, :], 1.0).then_inc(ones_ready, 1)
                pool.memset(mid[1][:, FT - 1, :], 1.0).then_inc(ones_ready, 1)

                def gather(i, m, first):
                    n, x, u = i * IT + m, m // 2, m % 2
                    if m % 2 == 0:
                        if not first or x:
                            pool.wait_ge(y_added, 16 * HT * (n - 2))
                        pool.tensor_copy(idx[x][:, :], slots[:, bass.ds(GS * i + x, 1), :].rearrange(
                            "p e k -> p (e k)")).then_inc(idx_ready, 1)
                        hold(pool, idx_ready, GS * i + x + 1, passed)
                    if not first or m >= 2:
                        pool.wait_ge(psT_ready, DH * (n - 1))
                        hold(pool, gate_ready, n - 1, passed)
                    for j in range(HT):
                        k = HT * (m % 2) + j
                        pool.indirect_dma_start(
                            out=g[u][:, j, :], out_offset=None, in_=xn_dram,
                            in_offset=bass.IndirectOffsetOnAxis(ap=idx[x][:, k:k + 1], axis=0)).then_inc(g_loaded[u], 16)

                def add(n, m):
                    x, u = m // 2, m % 2
                    pool.wait_ge(y_ready, 2 * n + 2)
                    for j in range(HT):
                        k = HT * (m % 2) + j
                        hold(pool, y_added, 16 * (HT * n + j), passed)
                        pool.indirect_dma_start(
                            out=x_out, out_offset=bass.IndirectOffsetOnAxis(ap=idx[x][:, k:k + 1], axis=0),
                            in_=y[u][:, j, :], in_offset=None, compute_op=ALU.add).then_inc(y_added, 16)

                def group(i, first=False):
                    for m in range(IT):
                        gather(i, m, first)
                        if not first or m >= 2:
                            add(i * IT + m - 2, (m - 2) % IT)

                group(0, first=True)
                with pool.Fori(1, NG) as i:
                    group(i)
                for m in (IT - 2, IT - 1):
                    add((NG - 1) * IT + m, m)
                pool.wait_ge(y_added, 16 * HT * NG * IT)

            @block.scalar
            def _(act):
                act.wait_ge(ones_ready, 2)
                act.wait_ge(bu_loaded, 16)

                def group(i, first=False):
                    act.wait_ge(mid_ready, i * IT * FT)
                    act.copy(bu[:, :], bu_all[:, bass.ds(i, 1), :].rearrange("p g f -> p (g f)")).then_inc(bu_ready, 1)
                    act.wait_ge(bu_ready, i + 1)
                    for m in range(IT):
                        n, u = i * IT + m, m % 2
                        if not first or m >= 2:
                            act.wait_ge(down_ready, 2 * (n - 1))
                        for f in range(FT):
                            r = P if f < FT - 1 else FR
                            act.wait_ge(up_ready, FT * n + f + 1)
                            act.activation(mid[u][0:r, f, :], psU[f % 3][0:r, :], ACT.Silu,
                                           bias=bu[0:r, f:f + 1]).then_inc(mid_ready, 1)

                group(0, first=True)
                with act.Fori(1, NG) as i:
                    group(i)

            @block.vector
            def _(dve):
                def take(i, m):
                    n, x, u = i * IT + m, m // 2, m % 2
                    for h in range(DH):
                        dve.wait_ge(psT_ready, DH * n + h + 1)
                        dve.tensor_copy(gT[u][:, h, :], psT[h][:, :]).then_inc(gT_ready, 1)
                    dve.tensor_scalar(gate[m][:, :], g[u][:, :, bass.ds(D + GS * i + x, 1)].rearrange("p j o -> p (j o)"),
                                      0.5, None, ALU.mult).then_inc(gate_ready, 1)

                def scale(n, m):
                    u = m % 2
                    dve.wait_ge(gate_ready, n + 1)
                    if isinstance(n, int) and n < 2:
                        pass
                    else:
                        dve.wait_ge(y_added, 16 * HT * (n - 1))
                    for k in range(2):
                        dve.wait_ge(down_ready, 2 * n + k + 1)
                        for j in range(2):
                            ins = dve.tensor_scalar(y[u][:, 2 * k + j, :], psD[k][:, j * D:(j + 1) * D],
                                                    gate[m][:, 2 * k + j:2 * k + j + 1], None, ALU.mult)
                        ins.then_inc(y_ready, 1)

                def group(i, first=False, last=False):
                    for m in range(IT):
                        if not (last and m == IT - 1):
                            take(i + (m + 1) // IT, (m + 1) % IT)
                        if not first or m:
                            scale(i * IT + m - 1, (m - 1) % IT)

                take(0, 0)
                group(0, first=True)
                with dve.Fori(1, NG - 1) as i:
                    group(i)
                group(NG - 1, last=True)
                scale(NG * IT - 1, IT - 1)

            @block.tensor
            def _(pe):
                def turn(i, m):
                    n, u = i * IT + m, m % 2
                    pe.wait_ge(g_loaded[u], 16 * HT * (2 * i + m // 2 + 1))
                    for h in range(DH):
                        pe.wait_ge(gT_ready, DH * n if isinstance(n, int) and not n else DH * (n - 1) + h + 1)
                        for j in range(HT):
                            ins = pe.transpose(psT[h][:, j * P:(j + 1) * P], g[u][:, j, h * P:(h + 1) * P], ident[:, :])
                        ins.then_inc(psT_ready, 1)

                def up(i, m):
                    n, u = i * IT + m, m % 2
                    pe.wait_ge(gT_ready, DH * n + DH)
                    pe.wait_ge(wup_loaded, 16 * i + 16)
                    for f in range(FT):
                        r = P if f < FT - 1 else FR
                        if not (isinstance(n, int) and n == 0 and f < 3):
                            pe.wait_ge(mid_ready, FT * n + f - 2)
                        for h in range(DH):
                            ins = pe.matmul(psU[f % 3][0:r, :], wup[:, h, f * P:f * P + r], gT[u][:, h, :],
                                            start=(h == 0), stop=(h == DH - 1))
                        ins.then_inc(up_ready, 1)

                def down(i, m):
                    n, x, u = i * IT + m, m // 2, m % 2
                    pe.wait_ge(mid_ready, FT * (n + 1))
                    pe.wait_ge(wdn_loaded, 48 * (GS * i + x + 1))
                    for k in range(2):
                        pe.wait_ge(y_ready, 0 if isinstance(n, int) and not n else 2 * (n - 1) + k + 1)
                        for j in range(2):
                            t = 2 * k + j
                            for f in range(FT):
                                r = P if f < FT - 1 else FR + 1
                                ins = pe.matmul(psD[k][:, j * D:(j + 1) * D], mid[u][0:r, f, t * P:(t + 1) * P],
                                                wdn[0:r, f, :], start=(f == 0), stop=(f == FT - 1))
                        ins.then_inc(down_ready, 1)

                def group(i, first=False, last=False):
                    for m in range(IT):
                        up(i, m)
                        if not (last and m == IT - 1):
                            turn(i + (m + 1) // IT, (m + 1) % IT)
                        if not first or m:
                            down(i - 1 if m == 0 else i, (m - 1) % IT)

                pe.wait_ge(ident_loaded, 16)
                turn(0, 0)
                group(0, first=True)
                with pe.Fori(1, NG - 1) as i:
                    group(i)
                group(NG - 1, last=True)
                down(NG - 1, IT - 1)




NH, HD = 16, 16
GH = 4
GROUPS = B * NH // GH
HG = NH // GH
AUG = 2 * HD
PARTS = 3
QREP = (3, 2, 1)
SK = 6 * HD


def qkv(nc, tag, x_in, qs, ks, vs, Wqkv, consts):
    with ExitStack() as ctx:
        a = Pool_(nc, ctx, tag)
        ident = a.sb("ident", [P, P])
        w = a.sb("w", [P, DH, 3 * D])
        neg_half = a.sb("neg_half", [P, LT])
        xt = [a.sb(f"xt{u}", [P, LT, D]) for u in range(2)]
        xn = a.sb("xn", [P, LT, D])
        xT = a.sb("xT", [P, DH, L])
        stats = [a.sb(f"stats{u}", [P, LT, 6]) for u in range(2)]
        mv = [a.sb(f"mv{u}", [P, LT, 2]) for u in range(2)]
        veps = [a.sb(f"veps{u}", [P, LT]) for u in range(2)]
        rstd = [a.sb(f"rstd{u}", [P, LT]) for u in range(2)]
        part = [[a.sb(f"part{u}_{k}", [P, BANK], bf16) for k in range(PARTS)] for u in range(4)]
        rest = [a.sb(f"rest{u}", [P, BANK]) for u in range(4)]
        va = [a.sb(f"va{u}", [P, HG, LT, GH, AUG]) for u in range(2)]
        psT = [a.ps(f"psT{k}", [P, BANK]) for k in range(2)]
        psQ = [a.ps(f"psQ{k}", [P, BANK]) for k in range(4)]
        psV = [a.ps(f"psV{k}", [P, BANK]) for k in range(2)]
        consts_loaded = a.sem("consts_loaded")
        x_loaded = a.sems("x_loaded")
        stats_ready, rstd_ready = a.sem("stats_ready"), a.sem("rstd_ready")
        xn_ready, psT_ready, psT_used = a.sem("xn_ready"), a.sems("psT_ready"), a.sems("psT_used")
        q_ready, v_ready, v_copied = a.sem("q_ready"), a.sem("v_ready"), a.sem("v_copied")
        part1, rest1, part2, part3 = (a.sem(n) for n in ("part1", "rest1", "part2", "part3"))
        part_stored, v_stored = a.sems("part_stored", 4), a.sems("v_stored")
        d_step, g_step, passed = a.sem("d_step"), a.sem("g_step"), a.sem("passed")
        QP = 2 * DH * 2

        with nc.Block() as block:
            @block.sync
            def _(sp):
                sp.dma_start(ident[:, :], consts["ident"]).then_inc(consts_loaded, 16)
                sp.dma_start(w[:, :, :], Wqkv.rearrange("(h p) e -> p h e", p=P)).then_inc(consts_loaded, 16)
                with sp.Fori(0, B // 2) as i:
                    for u in range(2):
                        sp.wait_ge(xn_ready, 2 * i)
                        sp.dma_start(xt[u][:, :, :], rows(x_in, 2 * i + u)).then_inc(x_loaded[u], 16)
                        for c in range(QP):
                            n = (2 * i + u) * QP + c
                            sp.wait_ge(part3, n + 1)
                            src = (qs, ks)[c // 4].rearrange("b k (h p) t -> b h k p t", p=P)
                            for k in range(PARTS):
                                dst = src[2 * i + u][(c // 2) % 2][k]
                                sp.dma_start(dst[:, (c % 2) * BANK:(c % 2 + 1) * BANK],
                                             part[c % 4][k][:, :]).then_inc(part_stored[c % 4], 16)
                        sp.wait_ge(v_copied, (2 * i + u) * 4 + 4)
                        sp.dma_start(vs.rearrange("b g p r -> b p g r")[2 * i + u],
                                     va[u][:, :, :, :, :].rearrange("p g t h a -> p g (t h a)")).then_inc(v_stored[u], 16)
                for u in range(4):
                    sp.wait_ge(part_stored[u], 16 * PARTS * 2 * B)
                for u in range(2):
                    sp.wait_ge(v_stored[u], 16 * (B // 2))

            @block.scalar
            def _(act):
                with act.Fori(0, B // 2) as i:
                    for u in range(2):
                        b = 2 * i + u
                        act.wait_ge(v_ready, 4 * b)
                        for k in range(2 * DH):
                            h, q = k // 2, k % 2
                            act.wait_ge(psT_ready[k % 2], 2 * b + k // 2 + 1)
                            act.copy(xT[:, h, q * BANK:(q + 1) * BANK], psT[k % 2][:, :]).then_inc(psT_used[k % 2], 1)
                        for c in range(QP):
                            n = b * QP + c
                            act.wait_ge(q_ready, n + 1)
                            act.wait_ge(part_stored[c % 4], 16 * PARTS * (2 * b + c // 4))
                            act.copy(part[c % 4][0][:, :], psQ[c % 4][:, :]).then_inc(part1, 1)
                            if c:
                                act.wait_ge(rest1, n)
                                act.copy(part[(c - 1) % 4][1][:, :], rest[(c - 1) % 4][:, :]).then_inc(part2, 1)
                        act.wait_ge(rest1, (b + 1) * QP)
                        act.copy(part[3][1][:, :], rest[3][:, :]).then_inc(part2, 1)

            @block.gpsimd
            def _(pool):
                link = Link(pool, g_step)
                for u in range(2):
                    link.inc(pool.memset(va[u][:, :, :, :, :], 1.0))
                link.step(pool.memset(neg_half[:, :], -0.5))
                with pool.Fori(0, B // 2) as i:
                    for u in range(2):
                        b = 2 * i + u
                        link.at(b + 3)
                        hold(pool, stats_ready, b + 1, passed)
                        norm_rstd(pool, link, mv[u], veps[u], rstd[u], neg_half, EPS, rstd_ready)
                        for c in range(QP):
                            pool.wait_ge(part2, b * QP + c + 1)
                            pool.tensor_tensor(part[c % 4][2][:, :], rest[c % 4][:, :], part[c % 4][1][:, :],
                                               ALU.subtract).then_inc(part3, 1)

            @block.tensor
            def _(pe):
                pe.wait_ge(consts_loaded, 32)
                with pe.Fori(0, B // 2) as i:
                    for u in range(2):
                        b = 2 * i + u
                        pe.wait_ge(xn_ready, b + 1)
                        transposes(pe, xn, psT, ident, psT_used, psT_ready, 2 * b)
                        for k in range(2):
                            pe.wait_ge(psT_used[k], 2 * b + 2)
                        for c in range(QP):
                            pe.wait_ge(rest1, b * QP + max(c - 3, 0) if c < 4 else b * QP + c - 3)
                            for h in range(DH):
                                ins = pe.matmul(psQ[c % 4][:, :], w[:, h, (c // 2) * P:(c // 2 + 1) * P],
                                                xT[:, h, (c % 2) * BANK:(c % 2 + 1) * BANK],
                                                start=(h == 0), stop=(h == DH - 1))
                            ins.then_inc(q_ready, 1)
                        for c in range(LT // 2):
                            pe.wait_ge(v_copied, 4 * b + max(c - 1, 0))
                            for j in range(2):
                                t = 2 * c + j
                                for h in range(DH):
                                    ins = pe.matmul(psV[c % 2][:, j * D:(j + 1) * D], xT[:, h, t * P:(t + 1) * P],
                                                    w[:, h, 2 * D:3 * D], start=(h == 0), stop=(h == DH - 1))
                            ins.then_inc(v_ready, 1)

            @block.vector
            def _(dve):
                link = Link(dve, d_step)
                dve.wait_ge(g_step, 3)
                with dve.Fori(0, B // 2) as i:
                    for u in range(2):
                        b = 2 * i + u
                        link.at(b * LT)
                        dve.wait_ge(x_loaded[u], 16 * i + 16)
                        norm_stats(dve, link, xt[u], stats[u], mv[u], stats_ready, passed)
                        dve.wait_ge(rstd_ready, b + 1)
                        dve.wait_ge(stats_ready, b + 1)
                        dve.wait_ge(psT_ready[1], 2 * b)
                        norm_apply(dve, xt[u], mv[u], rstd[u], xn, xn_ready)
                        for c in range(QP):
                            dve.wait_ge(part1, b * QP + c + 1)
                            dve.wait_ge(part3, b * QP + max(c - 3, 0))
                            dve.tensor_tensor(rest[c % 4][:, :], psQ[c % 4][:, :], part[c % 4][0][:, :],
                                              ALU.subtract).then_inc(rest1, 1)
                        dve.wait_ge(v_stored[u], 16 * i)
                        for c in range(LT // 2):
                            dve.wait_ge(v_ready, 4 * b + c + 1)
                            for g in range(HG):
                                ins = dve.tensor_copy(
                                    va[u][:, g, 2 * c:2 * c + 2, :, 0:HD],
                                    psV[c % 2][:, :].rearrange("p (j g h d) -> p g j h d", j=2, g=HG, d=HD)[:, g])
                            ins.then_inc(v_copied, 1)


def attention(nc, tag, qs, ks, vs, oT, consts):
    with ExitStack() as ctx:
        a = Pool_(nc, ctx, tag)
        identb = a.sb("identb", [P, P], bf16)
        later_k = a.sb("later_k", [P, P], bf16)
        later_q = a.sb("later_q", [P, P], bf16)
        pick = a.sb("pick", [P, P])
        qst = [a.sb(f"qst{u}", [P, GH, L], bf16) for u in range(HG)]
        kst = [a.sb(f"kst{u}", [P, GH, L], bf16) for u in range(HG)]
        va = [a.sb(f"va{u}", [P, LT, GH, AUG]) for u in range(HG)]
        NW = 8
        wt = [a.sb(f"wt{k}", [P, BANK]) for k in range(NW)]
        mx = a.sb("mx", [P, GH * LT])
        mrest = a.sb("mrest", [P, GH * LT])
        mp = a.sb("mp", [P, PARTS, GH * LT], bf16)
        mT = a.sb("mT", [PARTS * GH * LT, P], bf16)
        oS = [a.sb(f"oS{u}", [P, L]) for u in range(2)]
        rd = a.sb("rd", [P, L])
        on = [a.sb(f"on{u}", [P, L]) for u in range(2)]
        psM = [a.ps(f"psM{k}", [P, 2 * BANK]) for k in range(2)]
        psE = [a.ps(f"psE{k}", [P, BANK]) for k in range(2)]
        psO = a.ps("psO", [P, L])
        consts_loaded, ones_ready = a.sem("consts_loaded"), a.sem("ones_ready")
        loaded = a.sems("loaded", HG)
        m_ready, m_used = a.sem("m_ready"), a.sem("m_used")
        mp_ready, m_loaded = a.sem("mp_ready"), a.sem("m_loaded")
        e_ready, w_ready, w_used = a.sem("e_ready"), a.sem("w_ready"), a.sem("w_used")
        o_copied = a.sem("o_copied")
        on_ready, o_stored = a.sem("on_ready"), a.sems("o_stored")
        d_step, passed = a.sem("d_step"), a.sem("passed")

        UNITS = [(kt, max(q, kt * P), q + BANK) for kt in range(LT) for q in range(0, L, BANK) if q + BANK > kt * P]
        NU = len(UNITS)
        NE = NU * GH
        TILES_M = [(x, j) for j in reversed(range(LT)) for x in range(GH)]
        total_e, total_m = sum(q1 - q0 for _, q0, q1 in UNITS), sum(j + 1 for _, j in TILES_M)
        plan, done, k = [], 0, 0
        for kt, q0, q1 in UNITS:
            done += q1 - q0
            n = []
            while k < len(TILES_M) and sum(j + 1 for _, j in TILES_M[:k + 1]) <= 1.12 * total_m * done / total_e:
                n.append(k)
                k += 1
            plan.append(n)
        plan[-1] += list(range(k, len(TILES_M)))
        N_M = len(TILES_M)
        SUM_AT = len(plan[0])

        def base(g):
            return N_M + 1 if isinstance(g, int) and g == 0 else N_M + (N_M + 2) * g

        def all_steps(eng, step):
            step(0, 0, 0, first=True)
            with eng.Fori(0, B - 1) as b:
                for h in range(1, HG + 1):
                    step(HG * b + h, b + h // HG, h % HG)
            for h in range(1, HG):
                step(HG * (B - 1) + h, B - 1, h, last=(h == HG - 1))

        def sums_used(g):
            if isinstance(g, int) and g >= GROUPS - 2:
                return base(GROUPS - 1) + (g - (GROUPS - 2)) + 1
            return N_M + (N_M + 2) * (g + 1) + SUM_AT + 1

        with nc.Block() as block:
            @block.sync
            def _(sp):
                for dst, src in ((identb, "identb"), (later_k, "later_k"), (later_q, "later_q"), (pick, "pick")):
                    sp.dma_start(dst[:, :], consts[src]).then_inc(consts_loaded, 16)

                def load(b, hg):
                    heads = slice(hg * GH * HD, (hg + 1) * GH * HD)
                    row = 0
                    for p, rep in enumerate(QREP):
                        for r in range(rep):
                            for dst, src, which in ((qst, qs, p), (kst, ks, r)):
                                v = src[:, which, heads, :].rearrange("b (x d) t -> b d x t", d=HD)[b]
                                sp.dma_start(dst[hg][row:row + HD, :, :], v).then_inc(loaded[hg], 16)
                            row += HD
                    sp.dma_start(va[hg][:, :, :, :].rearrange("p t h a -> p (t h a)"), vs[:, hg][b]).then_inc(loaded[hg], 16)

                def maxima(g, hg):
                    sp.wait_ge(m_used, base(g))
                    n = GH * LT
                    for p in range(PARTS):
                        sp.dma_start(qst[hg][SK + p:SK + p + 1, :, :].rearrange("o x (j t) -> o (x j) t", t=P),
                                     mT[p * n:(p + 1) * n, :]).then_inc(m_loaded, 16)

                def store(g, b, hg):
                    u = hg % 2
                    hold(sp, on_ready, g + 1, passed)
                    for x in range(GH):
                        sp.dma_start(oT[b][(hg * GH + x) * HD:(hg * GH + x + 1) * HD, :],
                                     on[u][AUG * x:AUG * x + HD, :]).then_inc(o_stored[u], 16)

                def step(g, b, hg, first=False, last=False):
                    if not isinstance(g, int) or g + HG - 1 < GROUPS:
                        if not first:
                            hold(sp, w_used, NU * g, passed)
                        load(b + (hg + HG - 1) // HG, (hg + HG - 1) % HG)
                    if not last:
                        maxima(g + 1, (hg + 1) % HG)
                    if not first:
                        store(g - 1, b if hg else b - 1, (hg - 1) % HG)

                for hg in range(HG - 1):
                    load(0, hg)
                maxima(0, 0)
                all_steps(sp, step)
                store(GROUPS - 1, B - 1, HG - 1)
                for u in range(2):
                    sp.wait_ge(o_stored[u], 16 * GH * GROUPS // 2)

            @block.gpsimd
            def _(pool):
                for u in range(HG):
                    pool.memset(kst[u][SK:SK + 32, :, :], 1.0).then_inc(ones_ready, 1)

                def output(g, b, hg):
                    u = hg % 2
                    pool.wait_ge(m_used, sums_used(g))
                    pool.wait_ge(o_stored[u], 16 * GH * (2 * b + hg // 2))
                    pool.tensor_tensor(on[u][:, :], oS[u][:, :], rd[:, :], ALU.mult).then_inc(on_ready, 1)

                with pool.Fori(0, B - 1) as b:
                    for hg in range(HG):
                        output(HG * b + hg, b, hg)
                for hg in range(HG):
                    output(HG * (B - 1) + hg, B - 1, hg)

            @block.scalar
            def _(act):
                def copy_o(g, hg):
                    act.wait_ge(w_used, NU * (g + 1))
                    act.wait_ge(on_ready, g if hg == 0 else g - 1)
                    act.copy(oS[hg % 2][:, :], psO[:, :]).then_inc(o_copied, 1)

                def step(g, b, hg, first=False, last=False):
                    for n, (kt, q0, q1) in enumerate(UNITS):
                        k = NU * g + n
                        if not first or n >= 2:
                            act.wait_ge(w_used, k - 1)
                        for x in range(GH):
                            act.wait_ge(e_ready, k * GH + x + 1)
                            act.activation(wt[(n * GH + x) % NW][:, 0:q1 - q0], psE[x % 2][:, 0:q1 - q0], ACT.Exp,
                                           scale=HD ** -0.5).then_inc(w_ready, 1)
                        if n == 0 and not first:
                            copy_o(g - 1, (hg - 1) % HG)

                all_steps(act, step)
                copy_o(GROUPS - 1, HG - 1)

            @block.vector
            def _(dve):
                link = Link(dve, d_step)

                def maximum(start, parity, n, k):
                    x, j = TILES_M[k]
                    dve.wait_ge(m_ready, start + n + 1)
                    dve.tensor_reduce(mx[:, x * LT + j:x * LT + j + 1], psM[(parity + n) % 2][:, 0:(j + 1) * P],
                                      AX.X, ALU.max).then_inc(m_used, 1)

                def parts(start, parity, n, g):
                    link.at(3 * g)
                    dve.wait_ge(m_used, start + n)
                    link.step(dve.tensor_scalar(mp[:, 0, :], mx[:, :], -1.0, None, ALU.mult))
                    link.step(dve.scalar_tensor_tensor(mrest[:, :], mx[:, :], -1.0, mp[:, 0, :], ALU.mult, ALU.subtract))
                    link.step(dve.tensor_copy(mp[:, 1, :], mrest[:, :]))
                    dve.tensor_tensor(mp[:, 2, :], mrest[:, :], mp[:, 1, :], ALU.subtract).then_inc(mp_ready, 1)
                    dve.wait_ge(m_ready, start + n + 1)
                    dve.wait_ge(m_loaded, 16 * PARTS * g)
                    dve.tensor_copy(mT[:, :], psM[(parity + n) % 2][0:PARTS * GH * LT, 0:P]).then_inc(m_used, 1)

                def sums(start, parity, n, g):
                    dve.wait_ge(m_ready, start + n + 1)
                    dve.wait_ge(on_ready, g)
                    dve.reciprocal(rd[:, :], psM[(parity + n) % 2][:, :]).then_inc(m_used, 1)

                def step(g, b, hg, first=False, last=False):
                    start, parity, n = base(g), int(first), 0
                    for u in range(NU):
                        if u == 1 and not first:
                            sums(start, parity, n, g - 1)
                            n += 1
                        for k in [] if last else plan[u]:
                            maximum(start, parity, n, k)
                            n += 1
                    if not last:
                        parts(start, parity, n, g + 1)

                for k in range(N_M):
                    maximum(0, 0, k, k)
                parts(0, 0, N_M, 0)
                all_steps(dve, step)
                sums(base(GROUPS - 1), 0, 1, GROUPS - 1)

            @block.tensor
            def _(pe):
                def maximum(start, parity, n, k, hg):
                    x, j = TILES_M[k]
                    ps = psM[(parity + n) % 2]
                    if not isinstance(start, int) or start + n >= 2:
                        pe.wait_ge(m_used, start + n - 1)
                    for c in range(0, (j + 1) * P, BANK):
                        r = min(BANK, (j + 1) * P - c)
                        diag = c + r == (j + 1) * P
                        ins = pe.matmul(ps[:, c:c + r], qst[hg][0:SK, x, j * P:(j + 1) * P], kst[hg][0:SK, x, c:c + r],
                                        start=True, stop=not diag)
                        if diag:
                            ins = pe.matmul(ps[:, c + r - P:c + r], identb[:, :], later_k[:, :], start=False, stop=True)
                    ins.then_inc(m_ready, 1)

                def parts(start, parity, n, g):
                    pe.wait_ge(mp_ready, g + 1)
                    pe.wait_ge(m_used, start + n - 1)
                    pe.matmul(psM[(parity + n) % 2][0:PARTS * GH * LT, 0:P], mp[:, :, :].rearrange("p k n -> p (k n)"),
                              identb[:, :], start=True, stop=True).then_inc(m_ready, 1)

                def sums(start, parity, n, g, hg):
                    pe.wait_ge(o_copied, g + 1)
                    pe.wait_ge(m_used, start + n - 1)
                    for c in range(0, L, BANK):
                        ins = pe.matmul(psM[(parity + n) % 2][:, c:c + BANK], pick[:, :], oS[hg % 2][:, c:c + BANK],
                                        start=True, stop=True)
                    ins.then_inc(m_ready, 1)

                def scores(g, hg, n, first):
                    kt, q0, q1 = UNITS[n]
                    for x in range(GH):
                        if not first or n or x >= 2:
                            pe.wait_ge(w_ready, (NU * g + n) * GH + x - 1)
                        diag = q0 == kt * P
                        ins = pe.matmul(psE[x % 2][:, 0:q1 - q0], kst[hg][0:SK + PARTS, x, kt * P:(kt + 1) * P],
                                        qst[hg][0:SK + PARTS, x, q0:q1], start=True, stop=not diag)
                        if diag:
                            ins = pe.matmul(psE[x % 2][:, 0:P], identb[:, :], later_q[:, :], start=False, stop=True)
                        ins.then_inc(e_ready, 1)

                def values(g, hg, n):
                    kt, q0, q1 = UNITS[n]
                    pe.wait_ge(w_ready, (NU * g + n + 1) * GH)
                    for x in range(GH):
                        ins = pe.matmul(psO[AUG * x:AUG * (x + 1), q0:q1], va[hg][:, kt, x, :],
                                        wt[(n * GH + x) % NW][:, 0:q1 - q0], start=(kt == 0),
                                        stop=(kt == q1 // P - 1))
                    ins.then_inc(w_used, 1)

                def step(g, b, hg, first=False, last=False):
                    start, parity, m = base(g), int(first), 0
                    pe.wait_ge(m_loaded, 16 * PARTS * (g + 1))
                    if not last:
                        pe.wait_ge(loaded[(hg + 1) % HG], LOADS * (b + (hg + 1) // HG + 1))
                    for n in range(NU):
                        scores(g, hg, n, first)
                        if n == 0 and not first:
                            values(g - 1, (hg - 1) % HG, NU - 1)
                        if n == 1 and not first:
                            sums(start, parity, m, g - 1, (hg - 1) % HG)
                            m += 1
                        if n:
                            values(g, hg, n - 1)
                        for k in [] if last else plan[n]:
                            maximum(start, parity, m, k, (hg + 1) % HG)
                            m += 1
                    if not last:
                        parts(start, parity, m, g + 1)

                LOADS = 16 * (2 * sum(QREP) + 1)
                pe.wait_ge(consts_loaded, 16 * 4)
                pe.wait_ge(ones_ready, HG)
                pe.wait_ge(loaded[0], LOADS)
                for k in range(N_M):
                    maximum(0, 0, k, k, 0)
                parts(0, 0, N_M, 0)
                all_steps(pe, step)
                values(GROUPS - 1, HG - 1, NU - 1)
                sums(base(GROUPS - 1), 0, 1, GROUPS - 1, HG - 1)


def project_out(nc, tag, x_in, x_out, oT, Wout, bout):
    with ExitStack() as ctx:
        a = Pool_(nc, ctx, tag)
        w = a.sb("w", [P, DH, D])
        bb = a.sb("bb", [P, D])
        xt = [a.sb(f"xt{u}", [P, LT, D]) for u in range(2)]
        o = [a.sb(f"o{u}", [P, DH, L]) for u in range(2)]
        y = [a.sb(f"y{u}", [P, LT, D]) for u in range(2)]
        ps = [a.ps(f"ps{k}", [P, 2, D]) for k in range(4)]
        consts_loaded = a.sem("consts_loaded")
        x_loaded, o_loaded, y_stored = a.sems("x_loaded"), a.sems("o_loaded"), a.sems("y_stored")
        ps_ready, xb_ready, y_ready = a.sem("ps_ready"), a.sem("xb_ready"), a.sem("y_ready")
        with nc.Block() as block:
            @block.sync
            def _(sp):
                sp.dma_start(w[:, :, :], Wout.rearrange("(h p) e -> p h e", p=P)).then_inc(consts_loaded, 16)
                sp.dma_start(bb[:, :], bout.rearrange("(o e) -> o e", o=1).to_broadcast([P, D])).then_inc(consts_loaded, 16)
                with sp.Fori(0, B // 2) as i:
                    for u in range(2):
                        sp.wait_ge(y_ready, 4 * 2 * i)
                        sp.dma_start(xt[u][:, :, :], rows(x_in, 2 * i + u)).then_inc(x_loaded[u], 16)
                        sp.dma_start(o[u][:, :, :], oT.rearrange("b (h p) t -> b p h t", p=P)[2 * i + u]).then_inc(o_loaded[u], 16)

            @block.scalar
            def _(act):
                with act.Fori(0, B // 2) as i:
                    for u in range(2):
                        act.wait_ge(y_ready, 4 * (2 * i + u) + 4)
                        act.dma_start(rows(x_out, 2 * i + u), y[u][:, :, :]).then_inc(y_stored[u], 16)
                for u in range(2):
                    act.wait_ge(y_stored[u], 16 * (B // 2))

            @block.gpsimd
            def _(pool):
                pool.wait_ge(consts_loaded, 32)
                with pool.Fori(0, B // 2) as i:
                    for u in range(2):
                        pool.wait_ge(x_loaded[u], 16 * i + 16)
                        pool.wait_ge(y_stored[u], 16 * i)
                        pool.tensor_tensor(y[u][:, :, :], xt[u][:, :, :],
                                           bb[:, :].rearrange("p (o d) -> p o d", o=1).to_broadcast([P, LT, D]),
                                           ALU.add).then_inc(xb_ready, 1)

            @block.tensor
            def _(pe):
                pe.wait_ge(consts_loaded, 32)
                with pe.Fori(0, B // 2) as i:
                    for u in range(2):
                        pe.wait_ge(o_loaded[u], 16 * i + 16)
                        for k in range(LT // 2):
                            pe.wait_ge(y_ready, 4 * (2 * i + u))
                            for j in range(2):
                                t = 2 * k + j
                                for h in range(DH):
                                    ins = pe.matmul(ps[k][:, j, :], o[u][:, h, t * P:(t + 1) * P], w[:, h, :],
                                                    start=(h == 0), stop=(h == DH - 1))
                            ins.then_inc(ps_ready, 1)

            @block.vector
            def _(dve):
                with dve.Fori(0, B // 2) as i:
                    for u in range(2):
                        dve.wait_ge(xb_ready, 2 * i + u + 1)
                        for k in range(LT // 2):
                            dve.wait_ge(ps_ready, 4 * (2 * i + u) + k + 1)
                            dve.tensor_tensor(y[u][:, 2 * k:2 * k + 2, :], y[u][:, 2 * k:2 * k + 2, :], ps[k][:, :, :],
                                              ALU.add).then_inc(y_ready, 1)



def channel_mix(nc, tag, x_in, x_out, WrT, WkT, WvT, mu, consts):
    with ExitStack() as ctx:
        a = Pool_(nc, ctx, tag)
        ident = a.sb("ident", [P, P])
        wr, wk, wv = (a.sb(n, [P, DH, D]) for n in ("wr", "wk", "wv"))
        mus = a.sb("mus", [P, 2, DH])
        omu = a.sb("omu", [P, 2, DH])
        neg_half = a.sb("neg_half", [P, LT])
        xt = [a.sb(f"xt{u}", [P, LT, D]) for u in range(2)]
        xn = a.sb("xn", [P, LT, D])
        xT = a.sb("xT", [P, DH, 1 + L])
        stats = a.sb("stats", [P, LT, 6])
        mv = a.sb("mv", [P, LT, 2])
        veps = a.sb("veps", [P, LT])
        rstd = a.sb("rstd", [P, LT])
        before = a.sb("before", [P, 2, DH, L])
        mix = [a.sb(f"mix{u}", [P, 2, DH, L]) for u in range(2)]
        kr = [a.sb(f"kr{c}", [P, BANK]) for c in range(4)]
        ka = a.sb("ka", [P, DH, L])
        sg = a.sb("sg", [P, LT // 2, BANK])
        y = a.sb("y", [P, LT // 2, BANK])
        xo = [a.sb(f"xo{u}", [P, LT // 2, BANK]) for u in range(2)]
        psT = [a.ps(f"psT{k}", [P, BANK]) for k in range(2)]
        psK = [a.ps(f"psK{k}", [P, BANK]) for k in range(2)]
        psR = [a.ps(f"psR{k}", [P, BANK]) for k in range(2)]
        psV = [a.ps(f"psV{k}", [P, BANK]) for k in range(2)]
        consts_loaded = a.sem("consts_loaded")
        x_loaded, xo_stored = a.sems("x_loaded"), a.sems("xo_stored")
        stats_ready, rstd_ready = a.sem("stats_ready"), a.sem("rstd_ready")
        xn_ready, psT_ready, psT_used = a.sem("xn_ready"), a.sems("psT_ready"), a.sems("psT_used")
        omu_ready, before_ready, mix_ready = a.sem("omu_ready"), a.sem("before_ready"), a.sem("mix_ready")
        k_ready, kr_ready, ka_ready = a.sem("k_ready"), a.sem("kr_ready"), a.sem("ka_ready")
        r_ready, sg_ready, v_ready, y_ready = a.sem("r_ready"), a.sem("sg_ready"), a.sem("v_ready"), a.sem("y_ready")
        xo_ready = a.sem("xo_ready")
        d_step, g_step, passed = a.sem("d_step"), a.sem("g_step"), a.sem("passed")

        def all_sequences(eng, step):
            with eng.Fori(0, B // 2 - 1) as i:
                for u in range(2):
                    step(2 * i + u, u, i, False)
            for u in range(2):
                step(B - 2 + u, u, B // 2 - 1, u == 1)

        with nc.Block() as block:
            @block.sync
            def _(sp):
                for dst, src in ((ident[:, :], consts["ident"]), (mus[:, :, :].rearrange("p a h -> p (a h)"), mu),
                                 *((d_[:, :, :], s_.rearrange("(h p) d -> p h d", p=P))
                                   for d_, s_ in ((wr, WrT), (wk, WkT), (wv, WvT)))):
                    sp.dma_start(dst, src).then_inc(consts_loaded, 16)

                for u in range(2):
                    sp.dma_start(xt[u][:, :, :], rows(x_in, u)).then_inc(x_loaded[u], 16)
                with sp.Fori(1, B // 2) as i:
                    for u in range(2):
                        hold(sp, xo_ready, 4 * (2 * i + u - 1), passed)
                        sp.dma_start(xt[u][:, :, :], rows(x_in, 2 * i + u)).then_inc(x_loaded[u], 16)

            @block.gpsimd
            def _(pool):
                link = Link(pool, g_step)
                link.inc(pool.memset(xT[:, :, 0:1], 0.0))
                link.step(pool.memset(neg_half[:, :], -0.5))

                def rstds(b):
                    link.at(b + 2)
                    hold(pool, stats_ready, b + 1, passed)
                    norm_rstd(pool, link, mv, veps, rstd, neg_half, EPS, rstd_ready)

                def step(b, u, i, last):
                    if not last:
                        rstds(b + 1)
                    pool.wait_ge(v_ready, 4 * b)
                    for c in range(4):
                        pool.wait_ge(kr_ready, 4 * b + c + 1)
                        pool.tensor_tensor(ka[:, c // 2, (c % 2) * BANK:(c % 2 + 1) * BANK], kr[c][:, :], kr[c][:, :],
                                           ALU.mult).then_inc(ka_ready, 1)
                    pool.wait_ge(xo_stored[u], 16 * i)
                    for c in range(4):
                        pool.wait_ge(y_ready, 4 * b + c + 1)
                        pool.tensor_tensor(xo[u][:, c, :], y[:, c, :],
                                           xt[u][:, 2 * c:2 * c + 2, :].rearrange("p t d -> p (t d)"),
                                           ALU.add).then_inc(xo_ready, 1)

                rstds(0)
                all_sequences(pool, step)

            @block.scalar
            def _(act):
                act.wait_ge(omu_ready, 1)
                act.wait_ge(g_step, 2)

                def turned(b):
                    act.wait_ge(mix_ready, 4 * b)
                    for k in range(2 * DH):
                        h, q = k // 2, k % 2
                        act.wait_ge(psT_ready[k % 2], 2 * b + k // 2 + 1)
                        act.copy(xT[:, h, 1 + q * BANK:1 + (q + 1) * BANK], psT[k % 2][:, :]).then_inc(psT_used[k % 2], 1)
                    for k in range(2):
                        act.wait_ge(psT_used[k], 2 * b + 2)
                    for m in range(2):
                        for h in range(DH):
                            act.activation(before[:, m, h, :], xT[:, h, 0:L], ACT.Copy,
                                           scale=omu[:, m, h:h + 1]).then_inc(before_ready, 1)

                def step(b, u, i, last):
                    for c in range(4):
                        act.wait_ge(k_ready, 4 * b + c + 1)
                        act.wait_ge(ka_ready, 4 * b)
                        act.activation(kr[c][:, :], psK[c % 2][:, :], ACT.Relu).then_inc(kr_ready, 1)
                    for c in range(4):
                        act.wait_ge(r_ready, 4 * b + c + 1)
                        act.wait_ge(y_ready, 4 * b)
                        act.activation(sg[:, c, :], psR[c % 2][:, :], ACT.Sigmoid).then_inc(sg_ready, 1)
                    if not last:
                        turned(b + 1)
                    act.wait_ge(xo_ready, 4 * b + 4)
                    act.dma_start(rows(x_out, b), xo[u][:, :, :].rearrange("p c (j d) -> p (c j) d", d=D)).then_inc(xo_stored[u], 16)

                turned(0)
                all_sequences(act, step)
                for u in range(2):
                    act.wait_ge(xo_stored[u], 16 * (B // 2))

            @block.vector
            def _(dve):
                link = Link(dve, d_step)
                dve.wait_ge(consts_loaded, 16 * 5)
                dve.tensor_scalar(omu[:, :, :], mus[:, :, :], -1.0, 1.0, ALU.mult, ALU.add).then_inc(omu_ready, 1)

                def normed(b, u, i):
                    link.at(b * LT)
                    dve.wait_ge(x_loaded[u], 16 * i + 16)
                    norm_stats(dve, link, xt[u], stats, mv, stats_ready, passed)
                    dve.wait_ge(rstd_ready, b + 1)
                    dve.wait_ge(stats_ready, b + 1)
                    dve.wait_ge(psT_ready[1], 2 * b)
                    norm_apply(dve, xt[u], mv, rstd, xn, xn_ready)

                def mixed(b, u):
                    dve.wait_ge(r_ready, 0 if isinstance(b, int) and not b else 4 * b - 4)
                    for m in range(2):
                        for h in range(DH):
                            dve.wait_ge(before_ready, 4 * b + 2 * m + h + 1)
                            dve.scalar_tensor_tensor(mix[u][:, m, h, :], xT[:, h, 1:1 + L], mus[:, m, h:h + 1],
                                                     before[:, m, h, :], ALU.mult, ALU.add).then_inc(mix_ready, 1)

                def step(b, u, i, last):
                    if not last:
                        normed(b + 1, 1 - u, i + u)
                        mixed(b + 1, 1 - u)
                    dve.wait_ge(xo_ready, 4 * b)
                    for c in range(4):
                        dve.wait_ge(v_ready, 4 * b + c + 1)
                        dve.wait_ge(sg_ready, 4 * b + c + 1)
                        dve.scalar_tensor_tensor(y[:, c, :], psV[c % 2][:, :], 0.5, sg[:, c, :],
                                                 ALU.mult, ALU.mult).then_inc(y_ready, 1)

                normed(0, 0, 0)
                mixed(0, 0)
                all_sequences(dve, step)

            @block.tensor
            def _(pe):
                pe.wait_ge(consts_loaded, 16 * 5)

                def turn(b):
                    pe.wait_ge(xn_ready, b + 1)
                    transposes(pe, xn, psT, ident, psT_used, psT_ready, 2 * b)

                def by_row(c, ps, src, w, used, b, ready):
                    if c >= 2:
                        pe.wait_ge(used, 4 * b + c - 1)
                    else:
                        pe.wait_ge(used, 4 * b)
                    for j in range(2):
                        t = 2 * c + j
                        for h in range(DH):
                            ins = pe.matmul(ps[c % 2][:, j * D:(j + 1) * D], src[:, h, t * P:(t + 1) * P],
                                            w[:, h, :], start=(h == 0), stop=(h == DH - 1))
                    ins.then_inc(ready, 1)

                def step(b, u, i, last):
                    pe.wait_ge(mix_ready, 4 * b + 4)
                    for c in range(4):
                        pe.wait_ge(kr_ready, 4 * b + max(c - 1, 0))
                        for h in range(DH):
                            ins = pe.matmul(psK[c % 2][:, :], wk[:, h, (c // 2) * P:(c // 2 + 1) * P],
                                            mix[u][:, 1, h, (c % 2) * BANK:(c % 2 + 1) * BANK],
                                            start=(h == 0), stop=(h == DH - 1))
                        ins.then_inc(k_ready, 1)
                    for c in range(4):
                        by_row(c, psR, mix[u][:, 0], wr, sg_ready, b, r_ready)
                    if not last:
                        turn(b + 1)
                    pe.wait_ge(ka_ready, 4 * b + 4)
                    for c in range(4):
                        by_row(c, psV, ka, wv, y_ready, b, v_ready)

                turn(0)
                all_sequences(pe, step)



DI, NS, TAPS, DTR = 512, 16, 4, 64
IT_ = DI // P
XR = DTR + 2 * NS
EPS2 = 1e-6
SD = 32
NSTK = DI // SD
GD = P // NS
SG = SD // GD
NGRP = DI // GD


def mamba_inputs(nc, tag, x_in, x_res, stk, brep, crep, ucd, zsd, w, consts):
    with ExitStack() as ctx:
        a = Pool_(nc, ctx, tag)
        ident = a.sb("ident", [P, P])
        w_in = a.sb("w_in", [P, DH, 2 * DI])
        w_x = a.sb("w_x", [P, IT_, XR])
        w_dt = a.sb("w_dt", [XR, DI])
        pick_b, pick_c = a.sb("pick_b", [XR, P]), a.sb("pick_c", [XR, P])
        vec = a.sb("vec", [P, 2 * DH + IT_ * (TAPS + 2)])
        gamma = lambda h: vec[:, h:h + 1]
        beta = lambda h: vec[:, DH + h:DH + h + 1]
        at = 2 * DH
        tap = lambda j, k: vec[:, at + j * TAPS + k:at + j * TAPS + k + 1]
        conv_b = lambda j: vec[:, at + IT_ * TAPS + j:at + IT_ * TAPS + j + 1]
        dt_b = lambda j: vec[:, at + IT_ * (TAPS + 1) + j:at + IT_ * (TAPS + 1) + j + 1]
        neg_half = a.sb("neg_half", [P, LT])
        xt = [a.sb(f"xt{u}", [P, LT, D]) for u in range(2)]
        xn = a.sb("xn", [P, LT, D])
        xm = a.sb("xm", [P, LT, D])
        xr = a.sb("xr", [P, LT, D])
        stats = a.sb("stats", [P, LT, 6])
        mv = a.sb("mv", [P, LT, 2])
        mv2 = a.sb("mv2", [P, LT, 2])
        veps = a.sb("veps", [P, LT])
        rstd = a.sb("rstd", [P, LT])
        rstd2 = a.sb("rstd2", [P, LT])
        hT = a.sb("hT", [P, DH, L])
        ub = [a.sb(f"ub{u}", [P, TAPS - 1 + L]) for u in range(2)]
        cv = [a.sb(f"cv{u}", [P, L]) for u in range(2)]
        zs = [a.sb(f"zs{u}", [P, L]) for u in range(2)]
        uc = a.sb("uc", [P, IT_, L])
        xd = a.sb("xd", [XR, L])
        rep = [a.sb(f"rep{u}", [P, L]) for u in range(2)]
        ab = a.sb("ab", [P, L])
        ex = a.sb("ex", [P, L])
        ln = a.sb("ln", [P, L])
        pos = a.sb("pos", [P, L])
        dl = [a.sb(f"dl{q}", [P, L]) for q in range(2)]
        rest = [a.sb(f"rest{q}", [P, L]) for q in range(2)]
        part = [[a.sb(f"part{q}_{k}", [P, L], bf16) for k in range(PARTS)] for q in range(2)]
        psT = [a.ps(f"psT{k}", [P, BANK]) for k in range(2)]
        ps = [a.ps(f"ps{k}", [P, L]) for k in range(3)]
        sems = {n: a.sem(n) for n in (
            "consts_loaded", "stats_ready", "rstd_ready", "xn_ready", "xm_ready", "stats2_ready", "rstd2_ready",
            "xr_ready", "xr_stored", "p_ready", "ub_ready", "c0_ready", "cv_ready", "uc_ready", "uc_stored",
            "xd_ready", "rep_ready", "ab_ready", "ex_ready", "ln_ready", "pos_ready", "dl_ready",
            "du_ready", "part1", "rest1", "part2", "part3", "d_step", "g_step", "passed", "a_step")}
        S = sems
        zs_ready, zs_stored, rep_stored = a.sem("zs_ready"), a.sems("zs_stored"), a.sems("rep_stored")
        part_stored = a.sems("part_stored")
        x_loaded = a.sems("x_loaded")
        psT_ready, psT_used = a.sems("psT_ready"), a.sems("psT_used")
        NP_ = 2 * IT_ + 3 + IT_
        XD, BC, DT = 2 * IT_, 2 * IT_ + 1, 2 * IT_ + 3
        NW_ = 8

        with nc.Block() as block:
            @block.sync
            def _(sp):
                for dst, src in ((ident[:, :], consts["ident"]), (pick_b[:, :], consts["pick_b"]),
                                 (pick_c[:, :], consts["pick_c"]), (vec[:, :], w["vec"]),
                                 (w_in[:, :, :], w["w_in"].rearrange("(h p) e -> p h e", p=P)),
                                 (w_x[:, :, :], w["w_x"].rearrange("(h p) e -> p h e", p=P)),
                                 (w_dt[:, :], w["w_dt"])):
                    sp.dma_start(dst, src).then_inc(S["consts_loaded"], 16)
                for u in range(2):
                    sp.dma_start(xt[u][:, :, :], rows(x_in, u)).then_inc(x_loaded[u], 16)

                def step(b, i, u, more):
                    hold(sp, S["xr_ready"], b + 1, S["passed"])
                    sp.dma_start(rows(x_res, b), xr[:, :, :]).then_inc(S["xr_stored"], 16)
                    if more:
                        sp.dma_start(xt[u][:, :, :], rows(x_in, b + 2)).then_inc(x_loaded[u], 16)
                    for j in range(IT_):
                        hold(sp, zs_ready, IT_ * b + j + 1, S["passed"])
                        sp.dma_start(zsd[b][j * P:(j + 1) * P, :], zs[j % 2][:, :]).then_inc(zs_stored[j % 2], 16)
                    hold(sp, S["uc_ready"], IT_ * (b + 1), S["passed"])
                    sp.dma_start(ucd.rearrange("b (j p) t -> b p j t", p=P)[b], uc[:, :, :]).then_inc(S["uc_stored"], 16)
                    for k, dst in enumerate((brep, crep)):
                        hold(sp, S["rep_ready"], 2 * b + k + 1, S["passed"])
                        sp.dma_start(dst[b], rep[k][:, :]).then_inc(rep_stored[k], 16)
                    for j in range(IT_):
                        for q in range(2):
                            hold(sp, S["part3"], 2 * (IT_ * b + j) + q + 1, S["passed"])
                            for k in range(PARTS):
                                sp.dma_start(stk[b][q, k, j * P:(j + 1) * P, :], part[q][k][:, :]).then_inc(part_stored[q], 16)

                with sp.Fori(0, B // 2 - 1) as i:
                    for u in range(2):
                        step(2 * i + u, i, u, True)
                for u in range(2):
                    step(B - 2 + u, B // 2 - 1, u, False)
                for sem, n in ((S["xr_stored"], B), (zs_stored[0], 2 * B), (zs_stored[1], 2 * B), (S["uc_stored"], B),
                               (rep_stored[0], B), (rep_stored[1], B), (part_stored[0], PARTS * IT_ * B),
                               (part_stored[1], PARTS * IT_ * B)):
                    sp.wait_ge(sem, 16 * n)

            @block.gpsimd
            def _(pool):
                link = Link(pool, S["g_step"])
                for u in range(2):
                    link.inc(pool.memset(ub[u][:, 0:TAPS - 1], 0.0))
                link.step(pool.memset(neg_half[:, :], -0.5))

                def rstds(b):
                    link.at(2 * b + 3)
                    hold(pool, S["stats_ready"], b + 1, S["passed"])
                    norm_rstd(pool, link, mv, veps, rstd, neg_half, EPS, S["rstd_ready"])
                    hold(pool, S["stats2_ready"], b + 1, S["passed"])
                    norm_rstd(pool, link, mv2, veps, rstd2, neg_half, EPS2, S["rstd2_ready"])

                def residual(b, u):
                    rstds(b)
                    pool.wait_ge(S["xn_ready"], b + 1)
                    pool.wait_ge(S["xr_stored"], 16 * b)
                    pool.tensor_tensor(xr[:, :, :], xt[u][:, :, :], xn[:, :, :], ALU.add).then_inc(S["xr_ready"], 1)

                def step(b):
                    for j in range(IT_):
                        n = IT_ * b + j
                        pool.wait_ge(S["ln_ready"], n + 1)
                        pool.wait_ge(S["pos_ready"], n + 1)
                        pool.wait_ge(S["rest1"], 2 * n)
                        pool.tensor_tensor(dl[0][:, :], pos[:, :], ln[:, :], ALU.add).then_inc(S["dl_ready"], 1)
                        pool.wait_ge(S["dl_ready"], n + 1)
                        pool.tensor_tensor(dl[1][:, :], dl[0][:, :], uc[:, j, :], ALU.mult).then_inc(S["du_ready"], 1)
                        for q in range(2):
                            pool.wait_ge(S["part2"], 2 * n + q + 1)
                            pool.tensor_tensor(part[q][2][:, :], rest[q][:, :], part[q][1][:, :],
                                               ALU.subtract).then_inc(S["part3"], 1)

                residual(0, 0)
                with pool.Fori(0, B // 2 - 1) as i:
                    for u in range(2):
                        residual(2 * i + u + 1, 1 - u)
                        step(2 * i + u)
                residual(B - 1, 1)
                step(B - 2)
                step(B - 1)

            @block.scalar
            def _(act):
                act.wait_ge(S["consts_loaded"], 16 * 7)
                act.wait_ge(S["g_step"], 3)
                link = Link(act, S["a_step"])

                def step(b):
                    act.wait_ge(S["p_ready"], NP_ * b)
                    for k in range(2 * DH):
                        h, q = k // 2, k % 2
                        act.wait_ge(psT_ready[k % 2], 2 * b + k // 2 + 1)
                        act.activation(hT[:, h, q * BANK:(q + 1) * BANK], psT[k % 2][:, :], ACT.Identity,
                                       scale=gamma(h), bias=beta(h)).then_inc(psT_used[k % 2], 1)
                    for j in range(IT_):
                        u = j % 2
                        act.wait_ge(S["p_ready"], NP_ * b + 2 * j + 1)
                        act.wait_ge(zs_stored[u], 16 * (2 * b + j // 2))
                        act.activation(zs[u][:, :], ps[(2 * j) % 3][:, :], ACT.Silu).then_inc(zs_ready, 1)
                        act.wait_ge(S["p_ready"], NP_ * b + 2 * j + 2)
                        act.wait_ge(S["cv_ready"], IT_ * b + max(j - 1, 0))
                        act.copy(ub[u][:, TAPS - 1:], ps[(2 * j + 1) % 3][:, :]).then_inc(S["ub_ready"], 1)
                        act.wait_ge(S["uc_ready"], IT_ * b + max(j - 1, 0))
                        act.wait_ge(S["ub_ready"], IT_ * b + j + 1)
                        act.activation(cv[u][:, :], ub[u][:, 0:L], ACT.Copy, scale=tap(j, 0)).then_inc(S["c0_ready"], 1)
                        if j:
                            silu_u(b, j - 1)
                    silu_u(b, IT_ - 1)
                    act.wait_ge(S["p_ready"], NP_ * b + XD + 1)
                    act.copy(xd[:, :], ps[XD % 3][0:XR, :]).then_inc(S["xd_ready"], 1)
                    for k in range(2):
                        act.wait_ge(S["p_ready"], NP_ * b + BC + k + 1)
                        act.wait_ge(rep_stored[k], 16 * b)
                        act.copy(rep[k][:, :], ps[(BC + k) % 3][:, :]).then_inc(S["rep_ready"], 1)
                    for j in range(IT_):
                        n = IT_ * b + j
                        act.wait_ge(S["p_ready"], NP_ * b + DT + j + 1)
                        act.activation(ab[:, :], ps[(DT + j) % 3][:, :], ACT.Abs, bias=dt_b(j)).then_inc(S["ab_ready"], 1)
                        act.wait_ge(S["ab_ready"], n + 1)
                        act.activation(ex[:, :], ab[:, :], ACT.Exp, scale=-1.0).then_inc(S["ex_ready"], 1)
                        act.wait_ge(S["ex_ready"], n + 1)
                        act.wait_ge(S["dl_ready"], n)
                        act.activation(ln[:, :], ex[:, :], ACT.Ln, bias=1.0).then_inc(S["ln_ready"], 1)
                        for q in range(2):
                            act.wait_ge((S["dl_ready"], S["du_ready"])[q], n + 1)
                            act.wait_ge(part_stored[q], 16 * PARTS * n)
                            act.copy(part[q][0][:, :], dl[q][:, :]).then_inc(S["part1"], 1)

                def silu_u(b, j):
                    act.wait_ge(S["cv_ready"], IT_ * b + j + 1)
                    if j == 0:
                        act.wait_ge(S["uc_stored"], 16 * b)
                        act.wait_ge(S["du_ready"], IT_ * b)
                    act.activation(uc[:, j, :], cv[j % 2][:, :], ACT.Silu, bias=conv_b(j)).then_inc(S["uc_ready"], 1)

                with act.Fori(0, B) as b:
                    step(b)

            @block.vector
            def _(dve):
                link = Link(dve, S["d_step"])
                dve.wait_ge(S["consts_loaded"], 16 * 7)

                def norms(b, i, u):
                    link.at(b * 2 * LT)
                    dve.wait_ge(x_loaded[u], 16 * i + 16)
                    norm_stats(dve, link, xt[u], stats, mv, S["stats_ready"], S["passed"])
                    dve.wait_ge(S["rstd_ready"], b + 1)
                    dve.wait_ge(S["stats_ready"], b + 1)
                    dve.wait_ge(S["xr_ready"], b)
                    norm_apply(dve, xt[u], mv, rstd, xn, S["xn_ready"])
                    dve.wait_ge(S["xn_ready"], b + 1)
                    norm_stats(dve, link, xn, stats, mv2, S["stats2_ready"], S["passed"])
                    dve.wait_ge(S["rstd2_ready"], b + 1)
                    dve.wait_ge(S["stats2_ready"], b + 1)
                    dve.wait_ge(psT_ready[1], 2 * b)
                    norm_apply(dve, xn, mv2, rstd2, xm, S["xm_ready"])

                def step(b):
                    for j in range(IT_):
                        u = j % 2
                        dve.wait_ge(S["c0_ready"], IT_ * b + j + 1)
                        link.at(TAP0 + (TAPS - 2) * (IT_ * b + j))
                        for k in range(1, TAPS):
                            ins = dve.scalar_tensor_tensor(cv[u][:, :], ub[u][:, k:k + L], tap(j, k), cv[u][:, :],
                                                           ALU.mult, ALU.add)
                            if k < TAPS - 1:
                                ins.then_inc(S["c_step"], 1)
                                dve.wait_ge(S["c_step"], (TAPS - 2) * (IT_ * b + j) + k)
                        ins.then_inc(S["cv_ready"], 1)

                def deltas(b):
                    for j in range(IT_):
                        n = IT_ * b + j
                        dve.wait_ge(S["dl_ready"], n)
                        dve.wait_ge(S["ab_ready"], n + 1)
                        dve.tensor_scalar(pos[:, :], ps[(DT + j) % 3][:, :], dt_b(j), 0.0, ALU.add,
                                          ALU.max).then_inc(S["pos_ready"], 1)
                        for q in range(2):
                            dve.wait_ge(S["part1"], 2 * n + q + 1)
                            dve.wait_ge(S["part3"], 2 * n if q else 2 * n)
                            dve.tensor_tensor(rest[q][:, :], dl[q][:, :], part[q][0][:, :], ALU.subtract).then_inc(S["rest1"], 1)
                            dve.wait_ge(S["rest1"], 2 * n + q + 1)
                            dve.tensor_copy(part[q][1][:, :], rest[q][:, :]).then_inc(S["part2"], 1)

                TAP0 = 0
                S["c_step"] = a.sem("c_step")
                norms(0, 0, 0)
                with dve.Fori(0, B // 2 - 1) as i:
                    for u in range(2):
                        b = 2 * i + u
                        step(b)
                        norms(b + 1, i + u, 1 - u)
                        deltas(b)
                step(B - 2)
                norms(B - 1, B // 2 - 1, 1)
                deltas(B - 2)
                step(B - 1)
                deltas(B - 1)

            @block.tensor
            def _(pe):
                pe.wait_ge(S["consts_loaded"], 16 * 7)

                def free(b, n):
                    if n < 3:
                        pe.wait_ge(S["pos_ready"], IT_ * b)
                        return
                    m = n - 3
                    if m < 2 * IT_:
                        pe.wait_ge((zs_ready, S["ub_ready"])[m % 2], IT_ * b + m // 2 + 1)
                    elif m == XD:
                        pe.wait_ge(S["xd_ready"], b + 1)
                    elif m < DT:
                        pe.wait_ge(S["rep_ready"], 2 * b + m - BC + 1)
                    else:
                        pe.wait_ge(S["pos_ready"], IT_ * b + m - DT + 1)

                def step(b):
                    pe.wait_ge(S["xm_ready"], b + 1)
                    transposes(pe, xm, psT, ident, psT_used, psT_ready, 2 * b)
                    for k in range(2):
                        pe.wait_ge(psT_used[k], 2 * b + 2)
                    for n in range(2 * IT_):
                        free(b, n)
                        j = n // 2 + (0 if n % 2 else IT_)
                        for c in range(0, L, BANK):
                            for h in range(DH):
                                ins = pe.matmul(ps[n % 3][:, c:c + BANK], w_in[:, h, j * P:(j + 1) * P],
                                                hT[:, h, c:c + BANK], start=(h == 0), stop=(h == DH - 1))
                        ins.then_inc(S["p_ready"], 1)
                    free(b, XD)
                    pe.wait_ge(S["uc_ready"], IT_ * (b + 1))
                    for c in range(0, L, BANK):
                        for j in range(IT_):
                            ins = pe.matmul(ps[XD % 3][0:XR, c:c + BANK], w_x[:, j, :], uc[:, j, c:c + BANK],
                                            start=(j == 0), stop=(j == IT_ - 1))
                    ins.then_inc(S["p_ready"], 1)
                    pe.wait_ge(S["xd_ready"], b + 1)
                    for k, wk in enumerate([pick_b, pick_c] + [None] * IT_):
                        n = BC + k
                        free(b, n)
                        j = n - DT
                        for c in range(0, L, BANK):
                            ins = pe.matmul(ps[n % 3][:, c:c + BANK], wk[:, :] if wk is not None else w_dt[:, j * P:(j + 1) * P],
                                            xd[:, c:c + BANK], start=True, stop=True)
                        ins.then_inc(S["p_ready"], 1)

                with pe.Fori(0, B) as b:
                    step(b)


def mamba_scan(nc, tag, stk, brep, crep, yd, w_alog, consts):
    with ExitStack() as ctx:
        a = Pool_(nc, ctx, tag)
        spread = a.sb("spread", [PARTS * SD, SG, P], bf16)
        gather_d = a.sb("gather_d", [P, GD])
        alog = a.sb("alog", [P, NGRP])
        aexp = a.sb("aexp", [P, NGRP])
        aneg = a.sb("aneg", [P, NGRP])
        acur = [a.sb(f"acur{v}", [P, SG]) for v in range(2)]
        br = [a.sb(f"br{u}", [P, L]) for u in range(2)]
        cr = [a.sb(f"cr{u}", [P, L]) for u in range(2)]
        st = [a.sb(f"st{v}", [PARTS * SD, 2, L], bf16) for v in range(2)]
        dA = [a.sb(f"dA{k}", [P, L]) for k in range(2)]
        dB = [a.sb(f"dB{k}", [P, L]) for k in range(2)]
        hs = [a.sb(f"hs{k}", [P, L]) for k in range(4)]
        hc = [a.sb(f"hc{k}", [P, L]) for k in range(2 * SG)]
        ys = [a.sb(f"ys{v}", [P, L]) for v in range(2)]
        psD = a.ps("psD", [P, L])
        psU = [a.ps(f"psU{k}", [P, L]) for k in range(2)]
        psY = a.ps("psY", [P, L])
        consts_loaded, aneg_ready = a.sem("consts_loaded"), a.sem("aneg_ready")
        bc_loaded, st_loaded, ys_stored = a.sems("bc_loaded"), a.sems("st_loaded"), a.sems("ys_stored")
        acur_ready, d_ready, dA_ready = a.sem("acur_ready"), a.sem("d_ready"), a.sem("dA_ready")
        u_ready, dB_ready, hs_ready, hc_ready = a.sem("u_ready"), a.sem("dB_ready"), a.sem("hs_ready"), a.sem("hc_ready")
        y_ready, ys_ready, passed = a.sem("y_ready"), a.sem("ys_ready"), a.sem("passed")
        a_step = a.sem("a_step")

        def stacks(eng, step):
            with eng.Fori(0, B // 2) as i:
                for u in range(2):
                    b = 2 * i + u
                    with eng.Fori(0, NSTK // 2) as jj:
                        for v in range(2):
                            step(NSTK * b + 2 * jj + v, b, u, i, jj, v)

        with nc.Block() as block:
            @block.sync
            def _(sp):
                sp.dma_start(spread[:, :, :].rearrange("k r p -> k (r p)"), consts["spread"]).then_inc(consts_loaded, 16)
                sp.dma_start(gather_d[:, :], consts["gather_d"]).then_inc(consts_loaded, 16)
                sp.dma_start(alog[:, :], w_alog).then_inc(consts_loaded, 16)
                with sp.Fori(0, B // 2) as i:
                    for u in range(2):
                        b = 2 * i + u
                        hold(sp, hc_ready, NGRP * 2 * i, passed)
                        sp.dma_start(br[u][:, :], brep[b]).then_inc(bc_loaded[u], 16)
                        sp.dma_start(cr[u][:, :], crep[b]).then_inc(bc_loaded[u], 16)
                        with sp.Fori(0, NSTK // 2) as jj:
                            for v in range(2):
                                m = NSTK * b + 2 * jj + v
                                hold(sp, u_ready, SG * (NSTK * b + 2 * jj), passed)
                                for q in range(2):
                                    for k in range(PARTS):
                                        sp.dma_start(st[v][k * SD:(k + 1) * SD, q, :],
                                                     stk[:, q, k].rearrange("b (j p) t -> b j p t", p=SD)[b][2 * jj + v]).then_inc(st_loaded[v], 16)

            @block.scalar
            def _(act):
                link = Link(act, a_step)
                act.wait_ge(consts_loaded, 48)
                link.step(act.activation(aexp[:, :], alog[:, :], ACT.Exp))
                link.step(act.mul(aneg[:, :], aexp[:, :], -1.0))

                def step(m, b, u, i, jj, v):
                    act.copy(acur[v][:, :], aneg[:, bass.ds((2 * jj + v) * SG, SG)]).then_inc(acur_ready, 1)
                    act.wait_ge(acur_ready, m + 1)
                    for r in range(SG):
                        n = SG * m + r
                        act.wait_ge(d_ready, n + 1)
                        act.wait_ge(hs_ready, scans_before(b, jj, v, r))
                        act.activation(dA[r % 2][:, :], psD[:, :], ACT.Exp, scale=acur[v][:, r:r + 1]).then_inc(dA_ready, 1)
                    out(m, v, jj, b)

                def scans_before(b, jj, v, r):
                    k = SG * v + r
                    return SG * (NSTK * b + 2 * jj) + max(k - 1, 0)

                def out(m, v, jj, b):
                    act.wait_ge(y_ready, m + 1)
                    act.wait_ge(ys_stored[v], 16 * SG * ((NSTK // 2) * b + jj))
                    act.copy(ys[v][:, :], psY[:, :]).then_inc(ys_ready, 1)
                    for r in range(SG):
                        if r == 0:
                            hold(act, ys_ready, m + 1, passed)
                        act.dma_start(yd.rearrange("b (j r d) t -> (b j) r d t", r=SG, d=GD)[m][r],
                                      ys[v][32 * r:32 * r + GD, :]).then_inc(ys_stored[v], 16)

                stacks(act, step)
                for v in range(2):
                    act.wait_ge(ys_stored[v], 16 * SG * B * NSTK // 2)

            @block.tensor
            def _(pe):
                pe.wait_ge(consts_loaded, 48)

                def step(m, b, u, i, jj, v):
                    pe.wait_ge(st_loaded[v], 96 * ((NSTK // 2) * b + jj + 1))
                    for r in range(SG):
                        n = SG * m + r
                        pe.wait_ge(dA_ready, n)
                        for c in range(0, L, BANK):
                            ins = pe.matmul(psD[:, c:c + BANK], spread[:, r, :], st[v][:, 0, c:c + BANK], start=True, stop=True)
                        ins.then_inc(d_ready, 1)
                        k = SG * v + r
                        pe.wait_ge(dB_ready, SG * (NSTK * b + 2 * jj) + max(k - 1, 0))
                        for c in range(0, L, BANK):
                            ins = pe.matmul(psU[r % 2][:, c:c + BANK], spread[:, r, :], st[v][:, 1, c:c + BANK], start=True, stop=True)
                        ins.then_inc(u_ready, 1)
                    pe.wait_ge(hc_ready, SG * (m + 1))
                    pe.wait_ge(ys_ready, m)
                    for c in range(0, L, BANK):
                        for r in range(SG):
                            ins = pe.matmul(psY[32 * r:32 * r + GD, c:c + BANK], gather_d[:, :],
                                            hc[SG * v + r][:, c:c + BANK], start=True, stop=True)
                    ins.then_inc(y_ready, 1)

                stacks(pe, step)

            @block.vector
            def _(dve):
                dve.memset(psY[:, :], 0.0).then_inc(aneg_ready, 1)

                def step(m, b, u, i, jj, v):
                    dve.wait_ge(bc_loaded[u], 32 * i + 32)
                    for r in range(SG):
                        n = SG * m + r
                        dve.wait_ge(u_ready, n + 1)
                        dve.tensor_tensor(dB[r % 2][:, :], psU[r % 2][:, :], br[u][:, :], ALU.mult).then_inc(dB_ready, 1)
                        dve.wait_ge(dB_ready, n + 1)
                        dve.wait_ge(dA_ready, n + 1)
                        k = SG * v + r
                        dve.wait_ge(hc_ready, SG * (NSTK * b + 2 * jj) + max(k - 3, 0))
                        dve.tensor_tensor_scan(hs[r][:, :], dA[r % 2][:, :], dB[r % 2][:, :], 0.0, ALU.mult,
                                               ALU.add).then_inc(hs_ready, 1)

                stacks(dve, step)

            @block.gpsimd
            def _(pool):
                def step(m, b, u, i, jj, v):
                    pool.wait_ge(y_ready, NSTK * b + 2 * jj)
                    for r in range(SG):
                        pool.wait_ge(hs_ready, SG * m + r + 1)
                        pool.tensor_tensor(hc[SG * v + r][:, :], hs[r][:, :], cr[u][:, :], ALU.mult).then_inc(hc_ready, 1)

                stacks(pool, step)


def mamba_output(nc, tag, x_res, x_out, yd, ucd, zsd, w_outT, d_vec):
    with ExitStack() as ctx:
        a = Pool_(nc, ctx, tag)
        w = a.sb("w", [P, IT_, D])
        dv = a.sb("dv", [P, IT_])
        y = [a.sb(f"y{u}", [P, IT_, L]) for u in range(2)]
        uc = [a.sb(f"uc{u}", [P, IT_, L]) for u in range(2)]
        zs = [a.sb(f"zs{u}", [P, IT_, L]) for u in range(2)]
        xt = [a.sb(f"xt{u}", [P, LT, D]) for u in range(2)]
        ps = [a.ps(f"ps{k}", [P, 2, D]) for k in range(4)]
        consts_loaded = a.sem("consts_loaded")
        in_loaded, x_loaded, x_stored = a.sems("in_loaded"), a.sems("x_loaded"), a.sems("x_stored")
        skip_ready, gated_ready, ps_ready, x_ready = (a.sem(n) for n in ("skip_ready", "gated_ready", "ps_ready", "x_ready"))
        passed = a.sem("passed")
        with nc.Block() as block:
            @block.sync
            def _(sp):
                sp.dma_start(w[:, :, :], w_outT.rearrange("(h p) e -> p h e", p=P)).then_inc(consts_loaded, 16)
                sp.dma_start(dv[:, :], d_vec).then_inc(consts_loaded, 16)

                def load(b, u):
                    for dst, src in ((y, yd), (uc, ucd), (zs, zsd)):
                        sp.dma_start(dst[u][:, :, :], src.rearrange("b (j p) t -> b p j t", p=P)[b]).then_inc(in_loaded[u], 16)
                    sp.dma_start(xt[u][:, :, :], rows(x_res, b)).then_inc(x_loaded[u], 16)

                for u in range(2):
                    load(u, u)
                with sp.Fori(1, B // 2) as i:
                    for u in range(2):
                        hold(sp, x_stored[u], 16 * i, passed)
                        load(2 * i + u, u)

            @block.scalar
            def _(act):
                with act.Fori(0, B // 2) as i:
                    for u in range(2):
                        hold(act, x_ready, 4 * (2 * i + u) + 4, passed)
                        act.dma_start(rows(x_out, 2 * i + u), xt[u][:, :, :]).then_inc(x_stored[u], 16)
                for u in range(2):
                    act.wait_ge(x_stored[u], 16 * (B // 2))

            @block.gpsimd
            def _(pool):
                with pool.Fori(0, B // 2) as i:
                    for u in range(2):
                        for j in range(IT_):
                            pool.wait_ge(skip_ready, IT_ * (2 * i + u) + j + 1)
                            pool.tensor_tensor(y[u][:, j, :], y[u][:, j, :], zs[u][:, j, :], ALU.mult).then_inc(gated_ready, 1)

            @block.tensor
            def _(pe):
                pe.wait_ge(consts_loaded, 32)
                with pe.Fori(0, B // 2) as i:
                    for u in range(2):
                        b = 2 * i + u
                        pe.wait_ge(gated_ready, IT_ * (b + 1))
                        pe.wait_ge(x_ready, 4 * b)
                        for k in range(LT // 2):
                            for c in range(2):
                                t = 2 * k + c
                                for j in range(IT_):
                                    ins = pe.matmul(ps[k][:, c, :], y[u][:, j, t * P:(t + 1) * P], w[:, j, :],
                                                    start=(j == 0), stop=(j == IT_ - 1))
                            ins.then_inc(ps_ready, 1)

            @block.vector
            def _(dve):
                dve.wait_ge(consts_loaded, 32)

                def skips(b, i, u):
                    dve.wait_ge(in_loaded[u], 48 * i + 48)
                    for j in range(IT_):
                        dve.scalar_tensor_tensor(y[u][:, j, :], uc[u][:, j, :], dv[:, j:j + 1], y[u][:, j, :],
                                                 ALU.mult, ALU.add).then_inc(skip_ready, 1)

                def sums(b, i, u):
                    dve.wait_ge(x_loaded[u], 16 * i + 16)
                    for k in range(LT // 2):
                        dve.wait_ge(ps_ready, 4 * b + k + 1)
                        dve.tensor_tensor(xt[u][:, 2 * k:2 * k + 2, :], xt[u][:, 2 * k:2 * k + 2, :], ps[k][:, :, :],
                                          ALU.add).then_inc(x_ready, 1)

                skips(0, 0, 0)
                with dve.Fori(0, B // 2 - 1) as i:
                    for u in range(2):
                        skips(2 * i + u + 1, i + u, 1 - u)
                        sums(2 * i + u, i, u)
                skips(B - 1, B // 2 - 1, 1)
                sums(B - 2, B // 2 - 1, 0)
                sums(B - 1, B // 2 - 1, 1)


def constants():
    import numpy as np
    p, r = np.arange(P), np.arange(XR)
    same = (p[:, None] // 16 == p[None, :] // 16)
    col = np.arange(512)
    s, c = col // (E * 16), col % 16
    return {
        "ident": np.eye(P, dtype=np.float32),
        "same16": same.astype(np.float32),
        "below16": (same & (p[:, None] < p[None, :])).astype(np.float32),
        "identb": np.eye(P).astype(np.dtype("bfloat16")),
        "later_k": np.where(p[None, :] > p[:, None], -4e10, 0).astype(np.dtype("bfloat16")),
        "later_q": np.where(p[:, None] > p[None, :], -4e10, 0).astype(np.dtype("bfloat16")),
        "pick": ((p[:, None] // AUG == p[None, :] // AUG) & (p[:, None] % AUG == HD)).astype(np.float32),
        "pick_b": (r[:, None] == DTR + p[None, :] % NS).astype(np.float32),
        "pick_c": (r[:, None] == DTR + NS + p[None, :] % NS).astype(np.float32),
        "spread": np.concatenate([(r[:, None] % SD == GD * k + p[None, :] // NS) for k in range(SG)], 1).astype(np.dtype("bfloat16")),
        "gather_d": (p[:, None] // NS == p[None, :GD]).astype(np.float32),
        "pcol": p[:, None].astype(np.float32),
        "trow": np.broadcast_to((4 * c + s).astype(np.dtype("bfloat16")), (P, 512)).copy(),
    }


def laid_out(inputs):
    import numpy as np
    w = {k: np.asarray(v) for k, v in inputs.items()}
    out = {}
    out["x"] = w["L0_attn_x"].reshape(N_TOK, D)
    for n in ("Wr", "br", "W_up", "W_down", "b_down"):
        out[n] = w["L0_ffn_" + n]
    bu = np.zeros((NG, FT * P), np.float32)
    bu[:, :F] = w["L0_ffn_b_up"]
    out["b_up"] = bu.reshape(NG, FT, P).transpose(2, 0, 1).reshape(P, NG * FT)
    out["w_qkv"], out["w_out"], out["b_out"] = (w["L0_attn_" + n] for n in ("w_qkv", "w_out", "b_out"))
    for n in ("W_r", "W_k", "W_v"):
        out[n] = w["L1_ffn_" + n].T
    out["mu"] = np.stack([w["L1_ffn_mu_r"].reshape(DH, P), w["L1_ffn_mu_k"].reshape(DH, P)]).transpose(2, 0, 1).reshape(P, 2 * DH)
    m = {k[8:]: v for k, v in w.items() if k.startswith("L1_attn_")}
    out["w_in"] = m["in_proj_w"].T
    out["w_x"] = m["x_proj_w"].T
    w_dt = np.zeros((XR, DI), np.float32)
    w_dt[:DTR] = m["dt_proj_w"].T
    out["w_dt"] = w_dt
    out["w_mout"] = m["out_proj_w"].T
    tiles = lambda v: v.reshape(-1, P).T
    taps = m["conv_w"].reshape(IT_, P, TAPS).transpose(1, 0, 2).reshape(P, IT_ * TAPS)
    out["vec"] = np.concatenate([tiles(m["ln_gamma"]), tiles(m["ln_beta"]), taps, tiles(m["conv_b"]), tiles(m["dt_proj_b"])], 1)
    out["d_vec"] = tiles(m["D"])
    out["alog"] = m["A_log"].reshape(NGRP, P).T
    return {k: np.ascontiguousarray(v) for k, v in out.items()}


def build(nc, x, out, w, c):
    def dram(name, shape, dt=fp32):
        return nc.dram_tensor(name, shape, dt).ap()

    x1, x2, x3, x4, x5, res = (dram(n, [N_TOK, D]) for n in ("x1", "x2", "x3", "x4", "x5", "res"))
    table = dram("table", [N_TOK, ROW])
    scores = dram("scores", [P, 512])
    qs, ks = dram("qs", [B, PARTS, D, L], bf16), dram("ks", [B, PARTS, D, L], bf16)
    vs = dram("vs", [B, HG, P, LT * GH * AUG])
    oT = dram("oT", [B, D, L])
    stk = dram("stk", [B, 2, PARTS, DI, L], bf16)
    brep, crep = dram("brep", [B, P, L]), dram("crep", [B, P, L])
    ucd, zsd, yd = (dram(n, [B, DI, L]) for n in ("ucd", "zsd", "yd"))

    experts = [w[n] for n in ("Wr", "br", "W_up", "b_up", "W_down", "b_down")]
    mixing = [w[n] for n in ("W_r", "W_k", "W_v", "mu")]
    moe(nc, "m1", x, x1, table, scores, *experts, c)
    qkv(nc, "a1", x1, qs, ks, vs, w["w_qkv"], c)
    attention(nc, "a2", qs, ks, vs, oT, c)
    project_out(nc, "a3", x1, x2, oT, w["w_out"], w["b_out"])
    moe(nc, "m2", x2, x3, table, scores, *experts, c)
    channel_mix(nc, "c1", x3, x4, *mixing, c)
    mamba_inputs(nc, "s1", x4, res, stk, brep, crep, ucd, zsd, w, c)
    mamba_scan(nc, "s2", stk, brep, crep, yd, w["alog"], c)
    mamba_output(nc, "s3", res, x5, yd, ucd, zsd, w["w_mout"], w["d_vec"])
    channel_mix(nc, "c2", x5, out, *mixing, c)


def kernel(**inputs):
    import numpy as np
    import concourse.bacc as bacc
    from concourse.bass_utils import run_bass_kernel_spmd

    nc = bacc.Bacc("TRN2", target_bir_lowering=False, num_devices=1)
    arrays = {}

    def given(name, a):
        arrays[name] = np.ascontiguousarray(a)
        return nc.dram_tensor(name, a.shape, mybir.dt.from_np(a.dtype), kind="ExternalInput").ap()

    c = {n: given("c_" + n, a) for n, a in constants().items()}
    w = {n: given("w_" + n, a) for n, a in laid_out(inputs).items()}
    out = nc.dram_tensor("out", [N_TOK, D], fp32, kind="ExternalOutput").ap()
    build(nc, w.pop("x"), out, w, c)
    r = run_bass_kernel_spmd(nc, [arrays], core_ids=[0])
    return r.results[0]["out"].reshape(B, L, D)
```
